# Optimizing a Trainium2 kernel written in Bass

```python
import numpy as np
import jax
import jax.numpy as jnp

def _softmax(x, axis=-1):
    return jax.nn.softmax(x, axis=axis)

def _gelu(x):
    return jax.nn.gelu(x, approximate=True)

def _silu(x):
    return jax.nn.silu(x)

def _sigmoid(x):
    return jax.nn.sigmoid(x)

def _layernorm(x, axis=-1, eps=1e-05):
    m = jnp.mean(x, axis=axis, keepdims=True)
    v = jnp.var(x, axis=axis, keepdims=True)
    return (x - m) / jnp.sqrt(v + eps)

def _scatter_add(tgt, idx, src, axis=0):
    return tgt.at[idx].add(src)

def _segment_sum(src, seg, n):
    return jax.ops.segment_sum(src, seg, n)
kernel_name = 'mk_seq_preln_d1_jaxref_r8_a942a0'

def setup_inputs(seed: int=0):
    np.random.seed(seed)
    _w = jnp.asarray

    def _L0_attn_setup():
        import jax, jax.numpy as jnp
        import numpy as np
        HEAD_SIZE = 64
        key = jax.random.key(seed)
        ks = jax.random.split(key, 5)
        B, N, D, H, E, O = (2, 256, 128, 16, HEAD_SIZE, 128)
        return {'query': jax.random.normal(ks[0], (B, N, D), dtype=jnp.float32), 'Wq': jax.random.normal(ks[1], (H, D, E), dtype=jnp.float32) / np.sqrt(D), 'Wk': jax.random.normal(ks[2], (H, D, E), dtype=jnp.float32) / np.sqrt(D), 'Wv': jax.random.normal(ks[3], (H, D, E), dtype=jnp.float32) / np.sqrt(D), 'Wp': jax.random.normal(ks[4], (H * E, O), dtype=jnp.float32) / np.sqrt(H * E), 'bp': jnp.zeros((O,), dtype=jnp.float32)}
    _L0_attn_in = _L0_attn_setup()

    def _L0_ffn_setup():
        import jax, jax.numpy as jnp
        import numpy as np
        LN_EPS = 1e-05

        def layer_norm(x, g, b):
            mu = jnp.mean(x, axis=-1, keepdims=True)
            var = jnp.mean(jnp.square(x - mu), axis=-1, keepdims=True)
            return (x - mu) * jax.lax.rsqrt(var + LN_EPS) * g + b

        def ternary_quant(w):
            scale = 1.0 / jnp.clip(jnp.mean(jnp.abs(w)), 1e-05)
            wq = jnp.clip(jnp.round(w * scale), -1.0, 1.0) / scale
            return w + jax.lax.stop_gradient(wq - w)
        key = jax.random.key(seed)
        ks = jax.random.split(key, 3)
        dim, hidden = (128, 512)
        B, S = (8, 128)
        x = jax.random.normal(ks[0], (B, S, dim), dtype=jnp.float32)
        w1 = jax.random.normal(ks[1], (hidden, dim), dtype=jnp.float32) * 0.02
        w2 = jax.random.normal(ks[2], (dim, hidden), dtype=jnp.float32) * 0.02
        return {'x': x, 'ln1_g': jnp.ones((dim,), jnp.float32), 'ln1_b': jnp.zeros((dim,), jnp.float32), 'w1': w1, 'b1': jnp.zeros((hidden,), jnp.float32), 'ln2_g': jnp.ones((hidden,), jnp.float32), 'ln2_b': jnp.zeros((hidden,), jnp.float32), 'w2': w2, 'b2': jnp.zeros((dim,), jnp.float32)}
    _L0_ffn_in = _L0_ffn_setup()
    _d = {'L0_attn_query': _L0_attn_in['query'], 'L0_attn_Wq': _L0_attn_in['Wq'], 'L0_attn_Wk': _L0_attn_in['Wk'], 'L0_attn_Wv': _L0_attn_in['Wv'], 'L0_attn_Wp': _L0_attn_in['Wp'], 'L0_attn_bp': _L0_attn_in['bp'], 'L0_ffn_ln1_g': _L0_ffn_in['ln1_g'], 'L0_ffn_ln1_b': _L0_ffn_in['ln1_b'], 'L0_ffn_w1': _L0_ffn_in['w1'], 'L0_ffn_b1': _L0_ffn_in['b1'], 'L0_ffn_ln2_g': _L0_ffn_in['ln2_g'], 'L0_ffn_ln2_b': _L0_ffn_in['ln2_b'], 'L0_ffn_w2': _L0_ffn_in['w2'], 'L0_ffn_b2': _L0_ffn_in['b2']}
    _x0 = _d['L0_attn_query']
    _d['L0_attn_query'] = jax.random.normal(jax.random.fold_in(jax.random.key(seed), 1), (32, 256, 128), dtype=_x0.dtype)
    del _x0
    return _d

def reference(L0_attn_query, L0_attn_Wq, L0_attn_Wk, L0_attn_Wv, L0_attn_Wp, L0_attn_bp, L0_ffn_ln1_g, L0_ffn_ln1_b, L0_ffn_w1, L0_ffn_b1, L0_ffn_ln2_g, L0_ffn_ln2_b, L0_ffn_w2, L0_ffn_b2):

    def _L0_attn_ref(query, Wq, Wk, Wv, Wp, bp):
        import jax, jax.numpy as jnp
        import numpy as np
        HEAD_SIZE = 64
        B, N, D = query.shape
        H, _, E = Wq.shape
        scale = 1.0 / jnp.sqrt(jnp.asarray(E, query.dtype))
        q = jnp.einsum('bnd,hde->bhne', query, Wq) * scale
        k = jnp.einsum('bmd,hde->bhme', query, Wk)
        v = jnp.einsum('bmd,hde->bhme', query, Wv)
        logits = jnp.einsum('bhne,bhme->bhnm', q, k)
        attn = jax.nn.softmax(logits, axis=-1)
        out = jnp.einsum('bhnm,bhme->bnhe', attn, v)
        out = jnp.swapaxes(out, -1, -2).reshape(B, N, E * H)
        return jnp.dot(out, Wp) + bp

    def _L0_ffn_ref(x, ln1_g, ln1_b, w1, b1, ln2_g, ln2_b, w2, b2):
        import jax, jax.numpy as jnp
        import numpy as np
        LN_EPS = 1e-05

        def layer_norm(x, g, b):
            mu = jnp.mean(x, axis=-1, keepdims=True)
            var = jnp.mean(jnp.square(x - mu), axis=-1, keepdims=True)
            return (x - mu) * jax.lax.rsqrt(var + LN_EPS) * g + b

        def ternary_quant(w):
            scale = 1.0 / jnp.clip(jnp.mean(jnp.abs(w)), 1e-05)
            wq = jnp.clip(jnp.round(w * scale), -1.0, 1.0) / scale
            return w + jax.lax.stop_gradient(wq - w)
        h = layer_norm(x, ln1_g, ln1_b)
        h = jnp.einsum('bsd,hd->bsh', h, ternary_quant(w1)) + b1
        h = jax.nn.gelu(h, approximate=False)
        h = layer_norm(h, ln2_g, ln2_b)
        out = jnp.einsum('bsh,dh->bsd', h, ternary_quant(w2)) + b2
        return out
    x = L0_attn_query
    x = x + _L0_attn_ref(_layernorm(x, axis=-1), L0_attn_Wq, L0_attn_Wk, L0_attn_Wv, L0_attn_Wp, L0_attn_bp)
    x = x + _L0_ffn_ref(_layernorm(x, axis=-1), L0_ffn_ln1_g, L0_ffn_ln1_b, L0_ffn_w1, L0_ffn_b1, L0_ffn_ln2_g, L0_ffn_ln2_b, L0_ffn_w2, L0_ffn_b2)
    return x

_drawn_inputs = setup_inputs


def setup_inputs(seed=0):
    import zlib

    import numpy as np

    out = dict(_drawn_inputs(seed))
    spreads = {'L0_attn_bp': (0.0, 0.1),
     'L0_ffn_ln1_g': (1.0, 0.2),
     'L0_ffn_ln1_b': (0.0, 0.312),
     'L0_ffn_b1': (0.0, 0.1),
     'L0_ffn_ln2_g': (1.0, 0.2),
     'L0_ffn_ln2_b': (0.0, 0.294),
     'L0_ffn_b2': (0.0, 0.1)}
    factors = {}
    for name, (base, spread) in spreads.items():
        noise = np.random.default_rng([zlib.crc32(name.encode()), seed]).standard_normal(out[name].shape)
        drawn = base * np.exp(spread * noise) if base else spread * noise
        out[name] = jnp.asarray(drawn.astype(out[name].dtype))
    for name, factor in factors.items():
        out[name] = (out[name] * factor).astype(out[name].dtype)
    return out
```

```python
from contextlib import ExitStack

import concourse.bass as bass
import numpy as np
from concourse import mybir

F32, F16, BF16 = mybir.dt.float32, mybir.dt.float16, mybir.dt.bfloat16
ALU, ACT, AX = mybir.AluOpType, mybir.ActivationFunctionType, mybir.AxisListType
ROP = bass.bass_isa.ReduceOp

B, N, D = 32, 256, 128
H, E = 16, 64
F = 512
P = 128
NB = N // P
NT = B * NB
HC = H * E // P
FC = F // P
NH = B * H
EPS = 1e-5
TINY = 1e-20
VW = 130
GH = 4

Q_LEAD, MAX_LEAD, PV_LAG = 22, 19, 3
P_RING = 4
XT_RING = 3


class Signal:

    def __init__(self, sem, step=1):
        self.sem, self.step, self.count, self.at = sem, step, 0, {}


class Queues:

    def __init__(self):
        self.of = {name: [] for name in ("sp", "act", "pool", "dve", "pe")}
        self.waited = {}

    def do(self, engine, fn, signal=None, key=None):
        if signal is None:
            self.of[engine].append(fn)
            return
        signal.count += signal.step
        signal.at[key] = signal.count
        self.of[engine].append(lambda e: fn(e).then_inc(signal.sem, signal.step))

    def wait(self, engine, signal, key):
        value = signal.at[key]
        if self.waited.get((engine, signal.sem), 0) >= value:
            return
        self.waited[engine, signal.sem] = value
        self.of[engine].append(lambda e: e.wait_ge(signal.sem, value))

    def replay(self, engine, e):
        for fn in self.of[engine]:
            fn(e)


def layer(nc, x_in, wq_in, wk_in, wv_in, wp_in, bp_in, g1_in, lb1_in, w1_in, b1_in,
          g2_in, lb2_in, w2_in, b2_in, out):
    ctx = ExitStack()
    with ctx:
        def sb(name, shape, dt=F32):
            return ctx.enter_context(nc.sbuf_tensor(name, shape, dt))

        def signal(name, step=1):
            return Signal(ctx.enter_context(nc.semaphore(name)), step)

        q = Queues()
        do, wait = q.do, q.wait
        bank = [ctx.enter_context(nc.psum_tensor(f"bank{i}", [P, 512], F32)) for i in range(8)]

        X = sb("X", [P, NT, D])
        ident = sb("ident", [P, P])
        Mh, Ml = sb("Mh", [P, H, D], F16), sb("Ml", [P, H, D], F16)
        Wvh, Wvl = sb("Wvh", [P, H * E], F16), sb("Wvl", [P, H * E], F16)
        Wph, Wpl = sb("Wph", [P, HC, D], F16), sb("Wpl", [P, HC, D], F16)
        T1h, T1l = sb("T1h", [P, F], F16), sb("T1l", [P, F], F16)
        T2h, T2l = sb("T2h", [P, FC, D], F16), sb("T2l", [P, FC, D], F16)
        bias_rows = sb("bias_rows", [P, F], BF16)
        ones_bf = sb("ones_bf", [P, P], BF16)
        bias2 = sb("bias2", [P, D])
        bp_all = sb("bp_all", [P, D])
        largest = sb("largest", [P, 20])
        s_exp = sb("s_exp", [P, H])
        s_y, s_f1, s_f2 = sb("s_y", [P, 1]), sb("s_f1", [P, 1]), sb("s_f2", [P, 1])
        half = sb("half", [P, 2])
        xn = sb("xn", [P, NB, D])
        xTh = [sb(f"xTh{i}", [P, N], F16) for i in range(XT_RING)]
        xTl = [sb(f"xTl{i}", [P, N], F16) for i in range(XT_RING)]
        Qh = [sb(f"Qh{i}", [P, H, N], F16) for i in range(2)]
        Ql = [sb(f"Ql{i}", [P, H, N], F16) for i in range(2)]
        negmax = [sb(f"negmax{i}", [P, P]) for i in range(2)]
        shift = [sb(f"shift{i}", [H * NB, P], F16) for i in range(2)]
        V = [sb(f"V{i}", [P, NB, H, VW], F16) for i in range(2)]
        p32 = [sb(f"p32_{i}", [P, NB, N]) for i in range(P_RING)]
        ph = [sb(f"ph{i}", [P, NB, N], F16) for i in range(P_RING)]
        pl = [sb(f"pl{i}", [P, NB, N], F16) for i in range(P_RING)]
        o_part = [sb(f"o_part{i}", [P, NB, E]) for i in range(2)]
        O = [sb(f"O{i}", [P, NB, H, E]) for i in range(2)]
        rsum = [sb(f"rsum{i}", [P, NB, H]) for i in range(2)]
        OTh, OTl = sb("OTh", [P, HC, N], F16), sb("OTl", [P, HC, N], F16)
        st0, mv0 = sb("st0", [P, NB, 6]), sb("mv0", [P, NB, 2])
        ve0, r0 = sb("ve0", [P, NB]), sb("r0", [P, NB])
        st1, mv1 = sb("st1", [P, NB, 6]), sb("mv1", [P, NT, 2])
        ve1, r1 = sb("ve1", [P, NT]), sb("r1", [P, NT])

        setup = ExitStack()

        def tmp(name, shape, dt=F32):
            return setup.enter_context(nc.sbuf_tensor(name, shape, dt))

        W = tmp("W", [P, 3, H * E])
        Wlast = tmp("Wlast", [P, 3, H * E])
        WT = O[1][:, :, :, :].rearrange("p t h e -> p (t h e)").rearrange("p (i c d) -> p i c d", i=2, c=HC)
        M32 = O[0][:, :, :, :].rearrange("p t h e -> p (t h e)").rearrange("p (h d) -> p h d", h=H)
        Wp = tmp("Wp", [P, HC, D])
        w1, w2 = tmp("w1", [P, FC, D]), tmp("w2", [P, F])
        g1, lb1, g2, lb2 = tmp("g1", [P, 1]), tmp("lb1", [P, 1]), tmp("g2", [P, FC]), tmp("lb2", [P, FC])
        b1_all = tmp("b1_all", [P, F])
        b2_all = tmp("b2_all", [P, D])
        ones = tmp("ones", [P, P])
        part = tmp("part", [P, 20])
        psums, sums = tmp("psums", [P, 2]), tmp("sums", [P, 2])
        inv = tmp("inv", [P, 20])
        clip, sc, rsc = tmp("clip", [P, 2]), tmp("sc", [P, 2]), tmp("rsc", [P, 2])
        gs1, gs2 = tmp("gs1", [P, 1]), tmp("gs2", [P, FC])
        inv_f1 = tmp("inv_f1", [P, 1])
        wT32 = [Wlast[:, 0, 0:F], Wlast[:, 0, F:2 * F]]
        above = [Wlast[:, 1, 0:F], Wlast[:, 1, F:2 * F]]
        below = [Wlast[:, 2, 0:F], Wlast[:, 2, F:2 * F]]
        tern = [tmp("tern1", [P, F]), tmp("tern2", [P, F])]
        lbrep1, lbrep2 = tmp("lbrep1", [P, P]), tmp("lbrep2", [P, FC, P])
        bn = b1_all
        bpart = [tmp(f"bpart{i}", [P, F], BF16) for i in range(3)]

        s_wl = [signal(f"s_load_{n}", 16) for n in ("w", "last", "wp", "ffn", "rows")]
        s_xl = [signal(f"s_load_x{i}", 16) for i in range(9)]
        w_loaded, last_loaded, wp_loaded, ffn_loaded, rows_loaded = s_wl
        x_of = {}
        edges = [0, 2] + list(range(4, B + 1, 4))
        edges = sorted(set(edges))
        x_tok = x_in.rearrange("b (t p) d -> p (b t) d", p=P)

        def load(dst, src, sig, key, **kw):
            do("sp", lambda e: e.dma_start(dst, src, **kw), sig, key)

        for i, src in enumerate((wq_in, wk_in)):
            load(W[:, i, :].rearrange("p (h e) -> p h e", h=H), src.rearrange("h d e -> d h e"), w_loaded, "w")
        load(W[:, 2, :].rearrange("p (h e) -> p h e", h=H), wv_in.rearrange("h d e -> d h e"), w_loaded, "w")
        for i, src in enumerate((wq_in, wk_in, wv_in)):
            load(Wlast[:, i, :].rearrange("p (h e) -> p h e", h=H),
                 src[:, D - 1, :].partition_broadcast(P), last_loaded, "last")

        def load_x(c):
            a, z = edges[c], edges[c + 1]
            load(X[:, NB * a:NB * z, :], x_tok[:, NB * a:NB * z, :], s_xl[c], "x")
            for b in range(a, z):
                x_of[b] = s_xl[c]

        load_x(0)
        wp_v = wp_in.rearrange("(e c hh) o -> hh e c o", c=HC, hh=2)
        for hh in range(2):
            load(Wp[hh * E:(hh + 1) * E, :, :], wp_v[hh], wp_loaded, "wp")
        load(bp_all[:, :], bp_in.partition_broadcast(P), rows_loaded, "rows")
        load(w1[:, :, :], w1_in.rearrange("(c p) d -> p c d", p=P), ffn_loaded, "ffn")
        load(w2[:, :], w2_in, ffn_loaded, "ffn")
        load(g1[:, :], g1_in.rearrange("(p o) -> p o", o=1), ffn_loaded, "ffn")
        load(lb1[:, :], lb1_in.rearrange("(p o) -> p o", o=1), ffn_loaded, "ffn")
        load(g2[:, :], g2_in.rearrange("(c p) -> p c", p=P), ffn_loaded, "ffn", allow_slow_non_contiguous=True)
        load(lb2[:, :], lb2_in.rearrange("(c p) -> p c", p=P), ffn_loaded, "ffn", allow_slow_non_contiguous=True)
        load(b1_all[:, :], b1_in.partition_broadcast(P), rows_loaded, "rows")
        load(b2_all[:, :], b2_in.partition_broadcast(P), rows_loaded, "rows")
        for c in range(1, len(edges) - 1):
            load_x(c)

        s_const, s_id = signal("s_const"), signal("s_ident")
        do("pool", lambda e: e.memset(ident[:, :], 0.0), s_id, "zero")
        do("pool", lambda e: e.memset(half[:, :], -0.5), s_const, "half")
        wait("pool", s_id, "zero")
        do("pool", lambda e: e.affine_select(out=ident[:, :], in_=ident[:, :], compare_op=ALU.not_equal, fill=1.0,
                                             base=0, pattern=[[-1, P]], channel_multiplier=1), s_id, "ident")
        s_dc = signal("s_dve_const")
        for i in range(2):
            do("dve", lambda e, i=i: e.memset(negmax[i][:, :], 0.0))
            do("dve", lambda e, i=i: e.memset(V[i][:, :, :, 2 * E:2 * E + 1], 1.0))
        do("dve", lambda e: e.memset(xn[:, :, D - 1:D], 1.0))
        do("dve", lambda e: e.memset(ones[:, :], 1.0))
        do("dve", lambda e: e.memset(ones_bf[:, :], 1.0))
        do("dve", lambda e: e.memset(bias_rows[:, :], 0.0), s_dc, "consts")

        s_w = signal("s_weights")
        wait("dve", w_loaded, "w")
        wait("dve", last_loaded, "last")
        for i in range(3):
            do("dve", lambda e, i=i: e.tensor_tensor(W[:, i, :], W[:, i, :], Wlast[:, i, :], ALU.subtract), s_w, f"w{i}")

        s_wt, s_wtc, s_m, s_mc = signal("s_wt"), signal("s_wt_copied"), signal("s_m"), signal("s_m_copied")
        wait("pe", s_id, "ident")
        for i in range(2):
            wait("pe", s_w, f"w{i}")
            for k in range(2):
                ps = bank[2 * i + k]
                for c in range(4):
                    cc = 4 * k + c
                    do("pe", lambda e, ps=ps, c=c, cc=cc, i=i: e.transpose(
                        ps[:, c * P:(c + 1) * P], W[:, i, cc * P:(cc + 1) * P], ident[:, :]),
                        *((s_wt, (i, k)) if c == 3 else ()))
                wait("act", s_wt, (i, k))
                do("act", lambda e, ps=ps, i=i, k=k: e.activation(
                    WT[:, i, 4 * k:4 * k + 4, :], ps[:, :].rearrange("p (c d) -> p c d", c=4), ACT.Copy), s_wtc, (i, k))
        for k in range(4):
            ps, odd, c0 = bank[4 + k], k % 2, 4 * (k // 2)
            rows = slice(odd * E, (odd + 1) * E)
            wait("pe", s_wtc, (1, k // 2))
            for j in range(4):
                do("pe", lambda e, ps=ps, j=j, c0=c0, rows=rows: e.matmul(
                    ps[:, j * D:(j + 1) * D], WT[rows, 0, c0 + j, :], WT[rows, 1, c0 + j, :], start=True, stop=True),
                    *((s_m, k) if j == 3 else ()))
            wait("act", s_m, k)
            do("act", lambda e, ps=ps, odd=odd, c0=c0: e.activation(
                M32[:, :, :].rearrange("p (c hh) d -> p c hh d", hh=2)[:, c0:c0 + 4, odd, :],
                ps[:, :].rearrange("p (c d) -> p c d", c=4), ACT.Copy), s_mc, k)
        s_ft, s_fc = signal("s_ffn_t"), signal("s_ffn_copied")
        wait("pe", ffn_loaded, "ffn")
        for i in range(2):
            wait("pe", s_wtc, (0, i))
            for c in range(FC):
                src = w1[:, c, :] if i == 0 else w2[:, c * P:(c + 1) * P]
                do("pe", lambda e, i=i, c=c, src=src: e.transpose(bank[i][:, c * P:(c + 1) * P], src, ident[:, :]),
                   *((s_ft, i) if c == FC - 1 else ()))
            wait("act", s_ft, i)
            wait("act", s_w, "w2")
            do("act", lambda e, i=i: e.activation(wT32[i], bank[i][:, :], ACT.Copy), s_fc, i)

        def red(dst, src, op=ALU.max, axis=AX.X, key=None):
            do("dve", lambda e: e.tensor_reduce(dst, src, axis, op, apply_absolute_value=True),
               *((s_w, key) if key else ()))
        wait("dve", wp_loaded, "wp")
        wait("dve", ffn_loaded, "ffn")
        wait("dve", s_w, "w2")
        red(part[:, 16:17], W[:, 2, :])
        red(part[:, 17:18], Wp[:, :, :].rearrange("p c o -> p (c o)"))
        red(part[:, 18:19], g1[:, :])
        red(part[:, 19:20], g2[:, :])
        red(psums[:, 0:1], w1[:, :, :].rearrange("p c d -> p (c d)"), ALU.add)
        red(psums[:, 1:2], w2[:, :], ALU.add, key="psums")
        for k in range(4):
            wait("dve", s_mc, k)
        red(part[:, 0:H], M32[:, :, :], key="part")
        s_all = signal("s_all_reduced")
        wait("pool", s_w, "psums")
        do("pool", lambda e: e.partition_all_reduce(sums[:, :], psums[:, :], P, ROP.add), s_all, "sums")
        wait("pool", s_w, "part")
        do("pool", lambda e: e.partition_all_reduce(largest[:, :], part[:, :], P, ROP.max), s_all, "largest")

        n_step = [0]

        def step(fn):
            n_step[0] += 1
            do("dve", fn, s_w, n_step[0])
            wait("dve", s_w, n_step[0])

        wait("dve", s_all, "largest")
        step(lambda e: e.tensor_scalar(largest[:, :], largest[:, :], TINY, None, ALU.max))
        step(lambda e: e.reciprocal(inv[:, :], largest[:, :]))
        do("dve", lambda e: e.tensor_scalar(s_exp[:, :], largest[:, 0:H], float(E) ** -0.5, None, ALU.mult))
        do("dve", lambda e: e.tensor_tensor(s_y[:, :], largest[:, 16:17], largest[:, 17:18], ALU.mult))
        s_hi = signal("s_weight_hi")

        def split(src32, hi, lo, key):
            wait("act", s_w, n_step[0])
            do("act", lambda e: e.activation(hi, src32, ACT.Copy), s_hi, key)
            wait("dve", s_hi, key)
            do("dve", lambda e: e.tensor_tensor(lo, src32, hi, ALU.subtract), s_w, key)

        step(lambda e: e.tensor_tensor(M32[:, :, :], M32[:, :, :], inv[:, 0:H].unsqueeze(2).to_broadcast([P, H, D]), ALU.mult))
        split(M32[:, :, :], Mh[:, :, :], Ml[:, :, :], "M")
        step(lambda e: e.tensor_scalar(W[:, 2, :], W[:, 2, :], inv[:, 16:17], None, ALU.mult))
        split(W[:, 2, :], Wvh[:, :], Wvl[:, :], "Wv")
        step(lambda e: e.tensor_scalar(Wp[:, :, :], Wp[:, :, :], inv[:, 17:18], None, ALU.mult))
        split(Wp[:, :, :], Wph[:, :, :], Wpl[:, :, :], "Wp")

        wait("dve", s_fc, 0)
        wait("dve", s_fc, 1)
        wait("dve", s_all, "sums")
        step(lambda e: e.tensor_scalar(clip[:, :], sums[:, :], 1.0 / (F * D), 1e-5, ALU.mult, ALU.max))
        step(lambda e: e.reciprocal(sc[:, :], clip[:, :]))
        step(lambda e: e.reciprocal(rsc[:, :], sc[:, :]))
        for i in range(2):
            do("dve", lambda e, i=i: e.tensor_scalar(above[i], wT32[i], sc[:, i:i + 1], 0.5, ALU.mult, ALU.is_gt))
            step(lambda e, i=i: e.tensor_scalar(below[i], wT32[i], sc[:, i:i + 1], -0.5, ALU.mult, ALU.is_lt))
            step(lambda e, i=i: e.tensor_tensor(tern[i][:, :], above[i], below[i], ALU.subtract))
        do("dve", lambda e: e.tensor_tensor(s_f1[:, :], rsc[:, 0:1], largest[:, 18:19], ALU.mult))
        do("dve", lambda e: e.tensor_tensor(s_f2[:, :], rsc[:, 1:2], largest[:, 19:20], ALU.mult))
        do("dve", lambda e: e.tensor_scalar(gs2[:, :], g2[:, :], inv[:, 19:20], None, ALU.mult))
        do("dve", lambda e: e.tensor_scalar(lbrep1[:, :], ones[:, :], lb1[:, :], None, ALU.mult))
        for c in range(FC):
            do("dve", lambda e, c=c: e.tensor_scalar(lbrep2[:, c, :], ones[:, :], lb2[:, c:c + 1], None, ALU.mult))
        step(lambda e: e.tensor_scalar(gs1[:, :], g1[:, :], inv[:, 18:19], None, ALU.mult))
        s_fb = signal("s_ffn_bias")
        wait("pe", s_w, n_step[0])
        wait("pe", s_wtc, (1, 0))
        wait("pe", s_wtc, (1, 1))
        do("pe", lambda e: e.matmul(bank[2][:, :], lbrep1[:, :], tern[0][:, :], start=True, stop=True), s_fb, 0)
        for c in range(FC):
            do("pe", lambda e, c=c: e.matmul(bank[3][:, 0:D], lbrep2[:, c, :], tern[1][:, c * D:(c + 1) * D],
                                             start=c == 0, stop=c == FC - 1), *((s_fb, 1) if c == FC - 1 else ()))
        t32 = above
        do("dve", lambda e: e.tensor_scalar(t32[0], tern[0][:, :], gs1[:, :], None, ALU.mult))
        for c in range(FC):
            fn = (lambda e, c=c: e.tensor_scalar(t32[1][:, c * D:(c + 1) * D], tern[1][:, c * D:(c + 1) * D],
                                                 gs2[:, c:c + 1], None, ALU.mult))
            step(fn) if c == FC - 1 else do("dve", fn)
        split(t32[0], T1h[:, :], T1l[:, :], "T1")
        split(t32[1], T2h[:, :, :].rearrange("p c d -> p (c d)"), T2l[:, :, :].rearrange("p c d -> p (c d)"), "T2")
        wait("dve", s_fb, 1)
        wait("dve", rows_loaded, "rows")
        do("dve", lambda e: e.scalar_tensor_tensor(bias2[:, :], bank[3][:, 0:D], rsc[:, 1:2], b2_all[:, :], ALU.mult, ALU.add))
        step(lambda e: e.reciprocal(inv_f1[:, :], s_f1[:, :]))
        step(lambda e: e.scalar_tensor_tensor(bn[:, :], bank[2][:, :], rsc[:, 0:1], b1_all[:, :], ALU.mult, ALU.add))
        step(lambda e: e.tensor_scalar(bn[:, :], bn[:, :], inv_f1[:, :], None, ALU.mult))
        for i in range(3):
            step(lambda e, i=i: e.tensor_copy(bpart[i][:, :], bn[:, :]))
            if i < 2:
                step(lambda e, i=i: e.tensor_tensor(bn[:, :], bn[:, :], bpart[i][:, :], ALU.subtract))
            do("dve", lambda e, i=i: e.tensor_copy(bias_rows[32 * i:32 * i + 1, :], bpart[i][32 * i:32 * i + 1, :]),
               s_w, f"bias{i}")
        last_setup_w = "bias2"

        s_st, s_r0, s_xn, s_xbp = signal("s_ln_stats"), signal("s_ln_root"), signal("s_xn"), signal("s_x_plus_bp")
        s_misc = signal("s_misc_ready")
        s_mhi, s_mlo = signal("s_misc_hi"), signal("s_misc_lo")
        s_q, s_qhi, s_qlo = signal("s_q"), signal("s_q_hi"), signal("s_q_lo")
        s_ms, s_mx = signal("s_max_scores"), signal("s_max")
        s_sh = [signal(f"s_shift{i}", 16) for i in range(2)]
        s_sc, s_exp_done, s_ph, s_pl = signal("s_scores"), signal("s_exp"), signal("s_p_hi"), signal("s_p_lo")
        s_pv, s_o1, s_o, s_on = signal("s_pv"), signal("s_o_part"), signal("s_o"), signal("s_o_normal")
        s_x1 = signal("s_x1_stats")
        sc_bank, ms_bank, pv_bank, q_bank, misc = bank[0:2], bank[2:4], bank[4:6], bank[6], bank[7]

        def misc_free(engine="pe"):
            if s_mlo.count:
                s_mlo.at["last"] = s_mlo.count
                wait(engine, s_mlo, "last")

        def norm_stats(b):
            wait("dve", x_of[b], "x")
            if b:
                wait("dve", s_r0, b - 1)
            for t in range(NB):
                do("dve", lambda e, t=t: e.bn_stats(st0[:, t, :], X[:, NB * b + t, :]), s_st, ("st", b))
            wait("dve", s_st, ("st", b))
            for t in range(NB):
                do("dve", lambda e, t=t: e.bn_aggr(mv0[:, t, :], st0[:, t, :]), s_st, ("mv", b))

        def norm_root(b):
            wait("pool", s_st, ("mv", b))
            wait("pool", s_const, "half")
            do("pool", lambda e: e.tensor_scalar(ve0[:, :], mv0[:, :, 1], EPS, None, ALU.add), s_r0, ("ve", b))
            wait("pool", s_r0, ("ve", b))
            if b:
                wait("pool", s_xn, b - 1)
            do("pool", lambda e: e.tensor_tensor(r0[:, :], ve0[:, :], half[:, :], ALU.pow), s_r0, b)

        def norm_apply(b):
            wait("dve", s_r0, b)
            wait("dve", s_st, ("mv", b))
            if b:
                wait("dve", s_misc, ("xT", b - 1))
            for t in range(NB):
                do("dve", lambda e, t=t: e.tensor_scalar(xn[:, t, 0:D - 1], X[:, NB * b + t, 0:D - 1], mv0[:, t, 0:1],
                                                         r0[:, t:t + 1], ALU.subtract, ALU.mult), s_xn, b)

        def add_bp(b):
            wait("pool", s_xn, b)
            wait("pool", rows_loaded, "rows")
            tiles = X[:, NB * b:NB * b + NB, :]
            do("pool", lambda e: e.tensor_tensor(tiles, tiles, bp_all[:, :].unsqueeze(1).to_broadcast([P, NB, D]), ALU.add),
               s_xbp, b)

        def x_transposed(b):
            r = b % XT_RING
            misc_free()
            wait("pe", s_xn, b)
            wait("pe", s_dc, "consts")
            for t in range(NB):
                do("pe", lambda e, t=t: e.transpose(misc[:, t * P:(t + 1) * P], xn[:, t, :], ident[:, :]),
                   *((s_misc, ("xT", b)) if t == NB - 1 else ()))
            wait("act", s_misc, ("xT", b))
            if b >= XT_RING:
                wait("act", s_sc, H * (b - XT_RING) + H - 1)
                wait("dve", s_sc, H * (b - XT_RING) + H - 1)
            do("act", lambda e: e.activation(xTh[r][:, :], misc[:, 0:N], ACT.Copy), s_mhi, ("xT", b))
            wait("dve", s_mhi, ("xT", b))
            do("dve", lambda e: e.tensor_tensor(xTl[r][:, :], misc[:, 0:N], xTh[r][:, :], ALU.subtract), s_mlo, ("xT", b))

        def queries(g):
            b, h, r = g // H, g % H, (g // H) % XT_RING
            wait("pe", s_mlo, ("xT", b))
            wait("pe", s_w, "M")
            if g >= 2:
                wait("pe", s_qlo, g - 2)
            for j in range(2):
                o = q_bank[:, j * N:(j + 1) * N]
                for n, (m, xt) in enumerate(((Mh, xTh), (Mh, xTl), (Ml, xTh))):
                    do("pe", lambda e, o=o, m=m, xt=xt, j=j, n=n: e.matmul(
                        o, m[:, h + j, :], xt[r][:, :], start=n == 0, stop=n == 2),
                        *((s_q, g) if (j, n) == (1, 2) else ()))

        def queries_out(g):
            b, h = g // H, g % H
            wait("act", s_q, g)
            if b >= 2:
                wait("act", s_sc, g + 1 - 2 * H)
                wait("dve", s_sc, g + 1 - 2 * H)
            src = q_bank[:, :].rearrange("p (j n) -> p j n", j=2)
            hi, lo = Qh[b % 2][:, h:h + 2, :], Ql[b % 2][:, h:h + 2, :]
            do("act", lambda e: e.activation(hi, src, ACT.Copy), s_qhi, g)
            wait("dve", s_qhi, g)
            do("dve", lambda e: e.tensor_tensor(lo, src, hi, ALU.subtract), s_qlo, g)

        def max_scores(g):
            b, h = g // H, g % H
            wait("pe", s_qhi, g - g % 2)
            if g >= 2:
                wait("pe", s_mx, g - 2)
            for t in range(NB):
                do("pe", lambda e, t=t: e.matmul(ms_bank[g % 2][:, t * N:(t + 1) * N], Qh[b % 2][:, h, t * P:(t + 1) * P],
                                                 xTh[b % XT_RING][:, :], start=True, stop=True),
                   *((s_ms, g) if t == NB - 1 else ()))

        def max_out(g):
            b, h = g // H, g % H
            wait("dve", s_ms, g)
            if b >= 2:
                wait("dve", s_misc, ("shift", b - 2))
            do("dve", lambda e: e.tensor_reduce(negmax[b % 2][:, NB * h:NB * h + NB],
                                                ms_bank[g % 2][:, :].rearrange("p (t m) -> p t m", t=NB),
                                                AX.X, ALU.max, negate=True), s_mx, g)

        def shift_rows(b):
            misc_free()
            wait("pe", s_mx, H * b + H - 1)
            do("pe", lambda e: e.transpose(misc[:, 0:P], negmax[b % 2][:, :], ident[:, :]), s_misc, ("shift", b))
            wait("dve", s_misc, ("shift", b))
            if b >= 2:
                wait("dve", s_sh[b % 2], b - 2)
            do("dve", lambda e: e.tensor_copy(shift[b % 2][:, :], misc[0:H * NB, 0:P]), s_mlo, ("shift", b))
            wait("sp", s_mlo, ("shift", b))
            wait("sp", s_qlo, H * b + H - 2)
            do("sp", lambda e: e.dma_start(Qh[b % 2][D - 1:D, :, :].rearrange("p h (t n) -> p (h t) n", t=NB),
                                           shift[b % 2][:, :]), s_sh[b % 2], b)

        def scores(g):
            b, h, r = g // H, g % H, (g // H) % XT_RING
            wait("pe", s_sh[b % 2], b)
            wait("pe", s_qlo, g - g % 2)
            if g >= 2:
                wait("pe", s_exp_done, g - 2)
            for t in range(NB):
                o = sc_bank[g % 2][:, t * N:(t + 1) * N]
                for n, (xt, qq) in enumerate(((xTh, Qh), (xTh, Ql), (xTl, Qh))):
                    do("pe", lambda e, o=o, xt=xt, qq=qq, t=t, n=n: e.matmul(
                        o, xt[r][:, t * P:(t + 1) * P], qq[b % 2][:, h, :], start=n == 0, stop=n == 2),
                        *((s_sc, g) if (t, n) == (NB - 1, 2) else ()))

        def exps(g):
            i = g % P_RING
            wait("act", s_sc, g)
            if g >= P_RING:
                wait("act", s_pl, g - P_RING)
                wait("act", s_ph, g - P_RING)
            do("act", lambda e: e.activation(p32[i][:, :, :], sc_bank[g % 2][:, :].rearrange("p (t n) -> p t n", t=NB),
                                             ACT.Exp, scale=s_exp[:, g % H:g % H + 1]), s_exp_done, g)

        def split_p(g):
            i = g % P_RING
            wait("act", s_exp_done, g)
            if g >= P_RING:
                wait("act", s_pv, g - P_RING)
                wait("pool", s_pv, g - P_RING)
            do("act", lambda e: e.activation(ph[i][:, :, :], p32[i][:, :, :], ACT.Copy), s_ph, g)
            wait("pool", s_ph, g)
            do("pool", lambda e: e.tensor_tensor(pl[i][:, :, :], p32[i][:, :, :], ph[i][:, :, :], ALU.subtract), s_pl, g)

        def values(b, m, half_):
            r, cols = b % XT_RING, slice(half_ * 512, half_ * 512 + 512)
            h0 = half_ * 8
            misc_free()
            wait("pe", s_mlo, ("xT", b))
            wait("pe", s_w, "Wv")
            for n, (xt, w) in enumerate(((xTh, Wvh), (xTh, Wvl), (xTl, Wvh))):
                do("pe", lambda e, xt=xt, w=w, n=n: e.matmul(misc[:, :], xt[r][:, m * P:(m + 1) * P], w[:, cols],
                                                             start=n == 0, stop=n == 2),
                   *((s_misc, ("V", b, m, half_)) if n == 2 else ()))
            key = ("V", b, m, half_)
            src = misc[:, :].rearrange("p (h e) -> p h e", h=8)
            hi, lo = V[b % 2][:, m, h0:h0 + 8, E:2 * E], V[b % 2][:, m, h0:h0 + 8, 0:E]
            wait("act", s_misc, key)
            if b >= 2:
                wait("act", s_pv, H * (b - 2) + H - 1)
                wait("dve", s_pv, H * (b - 2) + H - 1)
            do("act", lambda e: e.activation(hi, src, ACT.Copy), s_mhi, key)
            wait("dve", s_mhi, key)
            do("dve", lambda e: e.tensor_tensor(lo, src, hi, ALU.subtract), s_mlo, key)

        def weighted(g):
            b, h, i = g // H, g % H, g % P_RING
            wait("pe", s_pl, g)
            for m in range(NB):
                wait("pe", s_mlo, ("V", b, m, h // 8))
            if g >= 2:
                wait("pe", s_o, g - 2)
            for t in range(NB):
                for m in range(NB):
                    for pp, lo in ((ph, 0), (pl, E)):
                        do("pe", lambda e, t=t, m=m, pp=pp, lo=lo: e.matmul(
                            pv_bank[g % 2][:, t * N + lo:t * N + 2 * E + 1], pp[i][:, m, t * P:(t + 1) * P],
                            V[b % 2][:, m, h, lo:2 * E + 1], start=m == 0 and lo == 0, stop=m == NB - 1 and lo == E),
                            *((s_pv, g) if (t, m, lo) == (NB - 1, NB - 1, E) else ()))

        def weighted_out(g):
            b, h = g // H, g % H
            src = pv_bank[g % 2][:, :].rearrange("p (t n) -> p t n", t=NB)
            wait("act", s_pv, g)
            if g >= 2:
                wait("act", s_o, g - 2)
            do("act", lambda e: e.activation(o_part[g % 2][:, :, :], src[:, :, E:2 * E], ACT.Copy), s_o1, g)
            wait("dve", s_o1, g)
            if b >= 2:
                wait("dve", s_misc, ("OT", b - 2, h // GH))
                wait("dve", s_on, (b - 2, h // GH))
            do("dve", lambda e: e.reciprocal(rsum[b % 2][:, :, h], src[:, :, 2 * E]))
            do("dve", lambda e: e.tensor_tensor(O[b % 2][:, :, h, :], src[:, :, 0:E], o_part[g % 2][:, :, :], ALU.add), s_o, g)

        def normalise(b, k):
            h0 = GH * k
            wait("pool", s_o, H * b + h0 + GH - 1)
            tile = O[b % 2][:, :, h0:h0 + GH, :]
            do("pool", lambda e: e.tensor_tensor(tile, tile, rsum[b % 2][:, :, h0:h0 + GH].unsqueeze(3)
                                                 .to_broadcast([P, NB, GH, E]), ALU.mult), s_on, (b, k))

        def outputs_transposed(b, k):
            misc_free()
            wait("pe", s_on, (b, k))
            key = ("OT", b, k)
            for cc in range(2):
                for t in range(NB):
                    h0 = GH * k + 2 * cc
                    do("pe", lambda e, cc=cc, t=t, h0=h0: e.transpose(
                        misc[:, (cc * NB + t) * P:(cc * NB + t + 1) * P],
                        O[b % 2][:, t, h0:h0 + 2, :].rearrange("p h e -> p (h e)"), ident[:, :]),
                        *((s_misc, key) if (cc, t) == (1, NB - 1) else ()))
            src = misc[:, :].rearrange("p (c n) -> p c n", c=2)
            hi, lo = OTh[:, 2 * k:2 * k + 2, :], OTl[:, 2 * k:2 * k + 2, :]
            wait("act", s_misc, key)
            if b:
                wait("act", s_misc, ("y", b - 1))
                wait("dve", s_misc, ("y", b - 1))
            do("act", lambda e: e.activation(hi, src, ACT.Copy), s_mhi, key)
            wait("dve", s_mhi, key)
            do("dve", lambda e: e.tensor_tensor(lo, src, hi, ALU.subtract), s_mlo, key)

        def project(b, t):
            if t == 0:
                misc_free()
                wait("pe", s_mlo, ("OT", b, H // GH - 1))
                wait("pe", s_w, "Wp")
            for c in range(HC):
                for n, (o, w) in enumerate(((OTh, Wph), (OTh, Wpl), (OTl, Wph))):
                    do("pe", lambda e, c=c, n=n, o=o, w=w: e.matmul(
                        misc[:, t * D:(t + 1) * D], o[:, c, t * P:(t + 1) * P], w[:, c, :],
                        start=(c, n) == (0, 0), stop=(c, n) == (HC - 1, 2)),
                        *((s_misc, ("y", b)) if (t, c, n) == (NB - 1, HC - 1, 2) else ()))

        def residual(b):
            wait("dve", s_misc, ("y", b))
            wait("dve", s_xbp, b)
            tiles = X[:, NB * b:NB * b + NB, :]
            do("dve", lambda e: e.scalar_tensor_tensor(tiles, misc[:, 0:NB * D].rearrange("p (t d) -> p t d", t=NB),
                                                       s_y[:, :], tiles, ALU.mult, ALU.add), s_mlo, ("y", b))

        def ffn_stats(b):
            wait("dve", s_mlo, ("y", b))
            for t in range(NB):
                do("dve", lambda e, t=t: e.bn_stats(st1[:, t, :], X[:, NB * b + t, :]), s_x1, ("st", b))
            wait("dve", s_x1, ("st", b))
            for t in range(NB):
                do("dve", lambda e, t=t: e.bn_aggr(mv1[:, NB * b + t, :], st1[:, t, :]), s_x1, ("mv", b))

        s_r1 = signal("s_ffn_root")

        def ffn_root(b):
            tl = slice(NB * b, NB * b + NB)
            wait("pool", s_x1, ("mv", b))
            do("pool", lambda e: e.tensor_scalar(ve1[:, tl], mv1[:, tl, 1], 1.0 + EPS, EPS * EPS, ALU.mult, ALU.add),
               s_r1, ("ve", b))
            wait("pool", s_r1, ("ve", b))
            do("pool", lambda e: e.tensor_tensor(r1[:, tl], ve1[:, tl], half[:, :], ALU.pow), s_r1, b)

        def batch_work(b, s):
            ok = lambda c: 0 <= c < B
            if s == 4 and ok(b + 2):
                norm_stats(b + 2)
                norm_root(b + 2)
            if s == 6 and ok(b + 2):
                norm_apply(b + 2)
                add_bp(b + 2)
            if s == 8 and ok(b + 2):
                x_transposed(b + 2)
            if s in (3, 4, 11, 12) and ok(b + 1):
                values(b + 1, s % 2 if s > 4 else 1 - s % 2, int(s > 4))
            if s == 13 and ok(b + 1):
                shift_rows(b + 1)
            for k, (at, back) in enumerate(((9, 0), (14, 0), (1, 1), (5, 1))):
                if s == at and ok(b - back):
                    outputs_transposed(b - back, k)
            for k, (at, back) in enumerate(((7, 0), (11, 0), (15, 0), (3, 1))):
                if s == at and ok(b - back):
                    normalise(b - back, k)
            if s in (6, 7) and ok(b - 1):
                project(b - 1, s - 6)
            if s == 7 and ok(b - 1):
                residual(b - 1)
            if s == 10 and ok(b - 1):
                ffn_stats(b - 1)
                ffn_root(b - 1)

        live = lambda g: 0 <= g < NH
        for t in range(-2 * H + 4, NH + H - 2):
            if live(t):
                scores(t)
                exps(t)
            if live(t - PV_LAG):
                weighted(t - PV_LAG)
                weighted_out(t - PV_LAG)
            if live(t):
                split_p(t)
            if live(t + MAX_LEAD):
                max_scores(t + MAX_LEAD)
            if t % 2 == 0 and live(t + Q_LEAD):
                queries(t + Q_LEAD)
                queries_out(t + Q_LEAD)
            if live(t + MAX_LEAD):
                max_out(t + MAX_LEAD)
            batch_work(t // H, t % H)
        setup.close()

        y = [sb(f"y{i}", [P, D]) for i in range(2)]
        yTh = [sb(f"yTh{i}", [P, P], F16) for i in range(2)]
        yTl = [sb(f"yTl{i}", [P, P], F16) for i in range(2)]
        a = [sb(f"a{i}", [P, F]) for i in range(2)]
        z = [sb(f"z{i}", [P, F]) for i in range(2)]
        zTh = [sb(f"zTh{i}", [P, FC, P], F16) for i in range(2)]
        zTl = [sb(f"zTl{i}", [P, FC, P], F16) for i in range(2)]
        st2 = [sb(f"st2_{i}", [P, 6]) for i in range(2)]
        mv2 = [sb(f"mv2_{i}", [P, 2]) for i in range(2)]
        ve2 = [sb(f"ve2_{i}", [P, 1]) for i in range(2)]
        r2 = [sb(f"r2_{i}", [P, 1]) for i in range(2)]
        nm2 = [sb(f"nm2_{i}", [P, 1]) for i in range(2)]
        s_y1, s_yt, s_yhi, s_ylo = signal("s_ffn_y"), signal("s_ffn_yT"), signal("s_ffn_y_hi"), signal("s_ffn_y_lo")
        s_pre, s_a, s_st2, s_r2, s_nm2 = (signal(f"s_ffn_{n}") for n in ("pre", "gelu", "stats2", "root2", "negmean"))
        s_z, s_zt, s_zhi, s_zlo = (signal(f"s_ffn_{n}") for n in ("z", "zT", "z_hi", "z_lo"))
        s_xb, s_f, s_out = signal("s_ffn_x_plus_bias"), signal("s_ffn_out"), signal("s_ffn_sum")
        s_store = signal("s_store", 16)
        yT_bank, pre_bank, z_bank, f_bank = bank[0:2], bank[2:4], bank[4:6], bank[6:8]
        STORE = 4

        def f_y(i):
            k = i % 2
            wait("dve", s_r1, i // NB)
            if i >= 2:
                wait("dve", s_yt, i - 2)
            do("dve", lambda e: e.tensor_scalar(y[k][:, :], X[:, i, :], mv1[:, i, 0:1], r1[:, i:i + 1],
                                                ALU.subtract, ALU.mult), s_y1, i)
            wait("pool", s_y1, i)
            do("pool", lambda e: e.tensor_tensor(X[:, i, :], X[:, i, :], bias2[:, :], ALU.add), s_xb, i)

        def f_yT(i):
            k = i % 2
            wait("pe", s_y1, i)
            if i >= 2:
                wait("pe", s_ylo, i - 2)
            do("pe", lambda e: e.transpose(yT_bank[k][:, 0:P], y[k][:, :], ident[:, :]), s_yt, i)
            wait("act", s_yt, i)
            if i >= 2:
                wait("act", s_pre, i - 2)
                wait("dve", s_pre, i - 2)
            do("act", lambda e: e.activation(yTh[k][:, :], yT_bank[k][:, 0:P], ACT.Copy), s_yhi, i)
            wait("dve", s_yhi, i)
            do("dve", lambda e: e.tensor_tensor(yTl[k][:, :], yT_bank[k][:, 0:P], yTh[k][:, :], ALU.subtract), s_ylo, i)

        def f_hidden(i):
            k = i % 2
            wait("pe", s_ylo, i)
            if i >= 2:
                wait("pe", s_a, i - 2)
            do("pe", lambda e: e.matmul(pre_bank[k][:, :], ones_bf[:, :], bias_rows[:, :], start=True, stop=False))
            do("pe", lambda e: e.matmul(pre_bank[k][:, :], yTh[k][:, :], T1h[:, :], start=False, stop=False))
            do("pe", lambda e: e.matmul(pre_bank[k][:, :], yTh[k][:, :], T1l[:, :], start=False, stop=False))
            do("pe", lambda e: e.matmul(pre_bank[k][:, :], yTl[k][:, :], T1h[:, :], start=False, stop=True), s_pre, i)
            wait("act", s_pre, i)
            if i >= 2:
                wait("act", s_z, i - 2)
                wait("act", s_st2, ("st", i - 2))
            do("act", lambda e: e.activation(a[k][:, :], pre_bank[k][:, :], ACT.Gelu, scale=s_f1[:, :]), s_a, i)
            wait("dve", s_a, i)
            if i >= 2:
                wait("dve", s_st2, ("mv", i - 2))
                wait("dve", s_r2, i - 2)
            do("dve", lambda e: e.bn_stats(st2[k][:, :], a[k][:, :]), s_st2, ("st", i))
            wait("dve", s_st2, ("st", i))
            if i >= 2:
                wait("dve", s_nm2, i - 2)
            do("dve", lambda e: e.bn_aggr(mv2[k][:, :], st2[k][:, :]), s_st2, ("mv", i))
            wait("pool", s_st2, ("mv", i))
            do("pool", lambda e: e.tensor_scalar(ve2[k][:, :], mv2[k][:, 1:2], EPS, None, ALU.add), s_r2, ("ve", i))
            wait("pool", s_r2, ("ve", i))
            if i >= 2:
                wait("pool", s_z, i - 2)
                wait("pool", s_nm2, i - 2)
            do("pool", lambda e: e.tensor_tensor(r2[k][:, :], ve2[k][:, :], half[:, 0:1], ALU.pow), s_r2, i)

        def f_norm(i):
            k = i % 2
            wait("dve", s_r2, i)
            if i >= 2:
                wait("dve", s_z, i - 2)
            do("dve", lambda e: e.scalar_tensor_tensor(nm2[k][:, :], mv2[k][:, 0:1], -1.0, r2[k][:, :], ALU.mult, ALU.mult),
               s_nm2, i)
            wait("act", s_nm2, i)
            if i >= 2:
                wait("act", s_zt, i - 2)
            do("act", lambda e: e.activation(z[k][:, :], a[k][:, :], ACT.Identity, scale=r2[k][:, :], bias=nm2[k][:, :]),
               s_z, i)

        def f_zT(i):
            k = i % 2
            wait("pe", s_z, i)
            if i >= 2:
                wait("pe", s_zlo, i - 2)
            for c in range(FC):
                do("pe", lambda e, c=c: e.transpose(z_bank[k][:, c * P:(c + 1) * P], z[k][:, c * P:(c + 1) * P], ident[:, :]),
                   *((s_zt, i) if c == FC - 1 else ()))
            wait("act", s_zt, i)
            if i >= 2:
                wait("act", s_f, i - 2)
                wait("dve", s_f, i - 2)
            src = z_bank[k][:, :].rearrange("p (c n) -> p c n", c=FC)
            do("act", lambda e: e.activation(zTh[k][:, :, :], src, ACT.Copy), s_zhi, i)
            wait("dve", s_zhi, i)
            do("dve", lambda e: e.tensor_tensor(zTl[k][:, :, :], src, zTh[k][:, :, :], ALU.subtract), s_zlo, i)

        def f_out(i):
            k = i % 2
            wait("pe", s_zlo, i)
            if i >= 2:
                wait("pe", s_out, i - 2)
            for c in range(FC):
                for n, (zz, w) in enumerate(((zTh, T2h), (zTh, T2l), (zTl, T2h))):
                    do("pe", lambda e, c=c, n=n, zz=zz, w=w: e.matmul(
                        f_bank[k][:, 0:D], zz[k][:, c, :], w[:, c, :], start=(c, n) == (0, 0), stop=(c, n) == (FC - 1, 2)),
                        *((s_f, i) if (c, n) == (FC - 1, 2) else ()))
            wait("dve", s_f, i)
            wait("dve", s_xb, i)
            do("dve", lambda e: e.scalar_tensor_tensor(X[:, i, :], f_bank[k][:, 0:D], s_f2[:, :], X[:, i, :],
                                                       ALU.mult, ALU.add), s_out, i)
            if i % STORE == STORE - 1:
                wait("sp", s_out, i)
                tl = slice(i + 1 - STORE, i + 1)
                do("sp", lambda e: e.dma_start(out.rearrange("b (t p) d -> p (b t) d", p=P)[:, tl, :], X[:, tl, :]),
                   s_store, i)

        for eng in ("pe", "pool"):
            wait(eng, s_w, last_setup_w)
        wait("pe", s_mlo, ("y", B - 1))
        for i in range(NT + 5):
            if i < NT:
                f_y(i)
                f_yT(i)
            if 0 <= i - 1 < NT:
                f_hidden(i - 1)
            if 0 <= i - 2 < NT:
                f_norm(i - 2)
            if 0 <= i - 3 < NT:
                f_zT(i - 3)
            if 0 <= i - 4 < NT:
                f_out(i - 4)
        wait("sp", s_store, NT - 1)

        block = ctx.enter_context(nc.Block())

        @block.sync
        def _(e):
            q.replay("sp", e)

        @block.scalar
        def _(e):
            q.replay("act", e)

        @block.gpsimd
        def _(e):
            q.replay("pool", e)

        @block.vector
        def _(e):
            q.replay("dve", e)

        @block.tensor
        def _(e):
            q.replay("pe", e)


_INS = ["L0_attn_query", "L0_attn_Wq", "L0_attn_Wk", "L0_attn_Wv", "L0_attn_Wp", "L0_attn_bp",
        "L0_ffn_ln1_g", "L0_ffn_ln1_b", "L0_ffn_w1", "L0_ffn_b1", "L0_ffn_ln2_g", "L0_ffn_ln2_b", "L0_ffn_w2", "L0_ffn_b2"]


def kernel(**inputs):
    from concourse import bacc
    from concourse.bass_utils import run_bass_kernel_spmd

    nc = bacc.Bacc("TRN2", target_bir_lowering=False, num_devices=1)
    arrays, args = {}, []
    for name in _INS:
        a = np.ascontiguousarray(inputs[name])
        arrays[f"in_{name}"] = a
        args.append(nc.dram_tensor(f"in_{name}", a.shape, mybir.dt.from_np(a.dtype), kind="ExternalInput").ap())
    result = nc.dram_tensor("result", (B, N, D), F32, kind="ExternalOutput").ap()
    layer(nc, *args, result)
    r = run_bass_kernel_spmd(nc, [arrays], core_ids=[0])
    return r.results[0]["result"]
```

```python
from contextlib import ExitStack

import concourse.bass as bass
import numpy as np
from concourse import mybir

F32, F16, BF16 = mybir.dt.float32, mybir.dt.float16, mybir.dt.bfloat16
ALU, ACT, AX = mybir.AluOpType, mybir.ActivationFunctionType, mybir.AxisListType
ROP = bass.bass_isa.ReduceOp

B, N, D = 32, 256, 128
H, E = 16, 64
F = 512
P = 128
NB = N // P
NT = B * NB
HC = H * E // P
FC = F // P
NH = B * H
EPS = 1e-5
TINY = 1e-20
VW = 130
GH = 4

Q_LEAD, MAX_LEAD, PV_LAG = 22, 19, 3
P_RING = 4
VALUE_STEPS = (3, 7, 11, 15)
PIECE_STEPS = (0, 6, 10, 14)
XT_RING = 3


class Signal:

    def __init__(self, sem, step=1):
        self.sem, self.step, self.count, self.at = sem, step, 0, {}


class Queues:

    def __init__(self):
        self.of = {name: [] for name in ("sp", "act", "pool", "dve", "pe")}
        self.waited = {}

    def do(self, engine, fn, signal=None, key=None):
        if signal is None:
            self.of[engine].append(fn)
            return
        signal.count += signal.step
        signal.at[key] = signal.count
        self.of[engine].append(lambda e: fn(e).then_inc(signal.sem, signal.step))

    def wait(self, engine, signal, key):
        value = signal.at[key]
        if self.waited.get((engine, signal.sem), 0) >= value:
            return
        self.waited[engine, signal.sem] = value
        self.of[engine].append(lambda e: e.wait_ge(signal.sem, value))

    def replay(self, engine, e):
        for fn in self.of[engine]:
            fn(e)


def layer(nc, x_in, wq_in, wk_in, wv_in, wp_in, bp_in, g1_in, lb1_in, w1_in, b1_in,
          g2_in, lb2_in, w2_in, b2_in, out):
    ctx = ExitStack()
    with ctx:
        def sb(name, shape, dt=F32):
            return ctx.enter_context(nc.sbuf_tensor(name, shape, dt))

        def signal(name, step=1):
            return Signal(ctx.enter_context(nc.semaphore(name)), step)

        q = Queues()
        do, wait = q.do, q.wait
        bank = [ctx.enter_context(nc.psum_tensor(f"bank{i}", [P, 512], F32)) for i in range(8)]

        X = sb("X", [P, NT, D])
        ident = sb("ident", [P, P])
        Mh, Ml = sb("Mh", [P, H, D], F16), sb("Ml", [P, H, D], F16)
        Wvh, Wvl = sb("Wvh", [P, H * E], F16), sb("Wvl", [P, H * E], F16)
        Wph, Wpl = sb("Wph", [P, HC, D], F16), sb("Wpl", [P, HC, D], F16)
        T1h, T1l = sb("T1h", [P, F], F16), sb("T1l", [P, F], F16)
        T2h, T2l = sb("T2h", [P, FC, D], F16), sb("T2l", [P, FC, D], F16)
        bias_rows = sb("bias_rows", [P, F], BF16)
        ones_bf = sb("ones_bf", [P, P], BF16)
        bias2 = sb("bias2", [P, D])
        bp_all = sb("bp_all", [P, D])
        largest = sb("largest", [P, 20])
        s_exp = sb("s_exp", [P, H])
        s_y, s_f1, s_f2 = sb("s_y", [P, 1]), sb("s_f1", [P, 1]), sb("s_f2", [P, 1])
        half = sb("half", [P, 2])
        xn = sb("xn", [P, NB, D])
        xTh = [sb(f"xTh{i}", [P, N], F16) for i in range(XT_RING)]
        xTl = [sb(f"xTl{i}", [P, N], F16) for i in range(XT_RING)]
        Qh = [sb(f"Qh{i}", [P, H, N], F16) for i in range(2)]
        Ql = [sb(f"Ql{i}", [P, H, N], F16) for i in range(2)]
        negmax = [sb(f"negmax{i}", [P, P]) for i in range(2)]
        shift = [sb(f"shift{i}", [H * NB, P], F16) for i in range(2)]
        V = [sb(f"V{i}", [P, NB, H, VW], F16) for i in range(2)]
        p32 = [sb(f"p32_{i}", [P, NB, N]) for i in range(P_RING)]
        ph = [sb(f"ph{i}", [P, NB, N], F16) for i in range(P_RING)]
        pl = [sb(f"pl{i}", [P, NB, N], F16) for i in range(P_RING)]
        o_part = [sb(f"o_part{i}", [P, NB, E]) for i in range(2)]
        O = [sb(f"O{i}", [P, NB, H, E]) for i in range(2)]
        rsum = [sb(f"rsum{i}", [P, NB, H]) for i in range(2)]
        OTh, OTl = sb("OTh", [P, HC, N], F16), sb("OTl", [P, HC, N], F16)
        st0, mv0 = sb("st0", [P, NB, 6]), sb("mv0", [P, NB, 2])
        ve0, r0 = sb("ve0", [P, NB]), sb("r0", [P, NB])
        st1, mv1 = sb("st1", [P, NB, 6]), sb("mv1", [P, NT, 2])
        ve1, r1 = sb("ve1", [P, NT]), sb("r1", [P, NT])

        setup = ExitStack()

        def tmp(name, shape, dt=F32):
            return setup.enter_context(nc.sbuf_tensor(name, shape, dt))

        W = tmp("W", [P, 3, H * E])
        Wv_last = tmp("Wv_last", [P, H * E])
        WT = O[1][:, :, :, :].rearrange("p t h e -> p (t h e)").rearrange("p (i c d) -> p i c d", i=2, c=HC)
        M32 = O[0][:, :, :, :].rearrange("p t h e -> p (t h e)").rearrange("p (h d) -> p h d", h=H)
        Wp = tmp("Wp", [P, HC, D])
        w1, w2 = tmp("w1", [P, FC, D]), tmp("w2", [P, F])
        g1, lb1, g2, lb2 = tmp("g1", [P, 1]), tmp("lb1", [P, 1]), tmp("g2", [P, FC]), tmp("lb2", [P, FC])
        b1_all, b2_all = tmp("b1_all", [P, F]), tmp("b2_all", [P, D])
        ones = tmp("ones", [P, P])
        part = tmp("part", [P, 20])
        psums, sums = tmp("psums", [P, 2]), tmp("sums", [P, 2])
        inv = tmp("inv", [P, 20])
        clip, sc, rsc = tmp("clip", [P, 2]), tmp("sc", [P, 2]), tmp("rsc", [P, 2])
        gs1, gs2, inv_f1 = tmp("gs1", [P, 1]), tmp("gs2", [P, FC]), tmp("inv_f1", [P, 1])
        above, below = [tmp(f"above{i}", [P, F]) for i in range(2)], [tmp(f"below{i}", [P, F]) for i in range(2)]
        tern = [tmp(f"tern{i}", [P, F]) for i in range(2)]
        lbrep1, lbrep2 = tmp("lbrep1", [P, P]), tmp("lbrep2", [P, FC, P])
        bn = b1_all
        bpart = [tmp(f"bpart{i}", [P, F], BF16) for i in range(3)]

        qk_loaded, v_loaded, wp_loaded, ffn_loaded, rows_loaded, bp_loaded = (
            signal(f"s_load_{n}", 16) for n in ("qk", "v", "wp", "ffn", "rows", "bp"))
        edges = [0, 2] + list(range(4, B + 1, 4))
        x_loaded = [signal(f"s_load_x{i}", 16) for i in range(len(edges) - 1)]
        x_of = {b: x_loaded[c] for c in range(len(edges) - 1) for b in range(edges[c], edges[c + 1])}
        x_tok = x_in.rearrange("b (t p) d -> p (b t) d", p=P)

        def load(dst, src, sig, key, **kw):
            do("sp", lambda e: e.dma_start(dst, src, **kw), sig, key)

        def load_w(i, src, sig):
            load(W[:, i, :].rearrange("p (h e) -> p h e", h=H), src.rearrange("h d e -> d h e"), sig, "w")

        def load_x(c):
            tl = slice(NB * edges[c], NB * edges[c + 1])
            load(X[:, tl, :], x_tok[:, tl, :], x_loaded[c], "x")

        load_w(0, wq_in, qk_loaded)
        load_w(1, wk_in, qk_loaded)
        load_x(0)
        load_w(2, wv_in, v_loaded)
        load(Wv_last[:, :].rearrange("p (h e) -> p h e", h=H), wv_in[:, D - 1, :].partition_broadcast(P), v_loaded, "w")
        load(bp_all[:, :], bp_in.partition_broadcast(P), bp_loaded, "bp")
        load_x(1)
        wp_v = wp_in.rearrange("(e c hh) o -> hh e c o", c=HC, hh=2)
        for hh in range(2):
            load(Wp[hh * E:(hh + 1) * E, :, :], wp_v[hh], wp_loaded, "wp")
        load(w1[:, :, :], w1_in.rearrange("(c p) d -> p c d", p=P), ffn_loaded, "ffn")
        load(w2[:, :], w2_in, ffn_loaded, "ffn")
        load(g1[:, :], g1_in.rearrange("(p o) -> p o", o=1), ffn_loaded, "ffn")
        load(lb1[:, :], lb1_in.rearrange("(p o) -> p o", o=1), ffn_loaded, "ffn")
        load(g2[:, :], g2_in.rearrange("(c p) -> p c", p=P), ffn_loaded, "ffn", allow_slow_non_contiguous=True)
        load(lb2[:, :], lb2_in.rearrange("(c p) -> p c", p=P), ffn_loaded, "ffn", allow_slow_non_contiguous=True)
        load(b1_all[:, :], b1_in.partition_broadcast(P), rows_loaded, "rows")
        load(b2_all[:, :], b2_in.partition_broadcast(P), rows_loaded, "rows")
        for c in range(2, len(edges) - 1):
            load_x(c)

        s_const, s_id = signal("s_const"), signal("s_ident")
        do("pool", lambda e: e.memset(ident[:, :], 0.0), s_id, "zero")
        do("pool", lambda e: e.memset(half[:, :], -0.5), s_const, "half")
        wait("pool", s_id, "zero")
        do("pool", lambda e: e.affine_select(out=ident[:, :], in_=ident[:, :], compare_op=ALU.not_equal, fill=1.0,
                                             base=0, pattern=[[-1, P]], channel_multiplier=1), s_id, "ident")
        s_dc = signal("s_dve_const")
        for i in range(2):
            do("dve", lambda e, i=i: e.memset(negmax[i][:, :], 0.0))
            do("dve", lambda e, i=i: e.memset(V[i][:, :, :, 2 * E:2 * E + 1], 1.0))
        do("dve", lambda e: e.memset(xn[:, :, D - 1:D], 1.0))
        do("dve", lambda e: e.memset(ones[:, :], 1.0))
        do("dve", lambda e: e.memset(ones_bf[:, :], 1.0))
        do("dve", lambda e: e.memset(bias_rows[:, :], 0.0), s_dc, "consts")

        s_w = signal("s_weights")
        s_hi = signal("s_weight_hi")
        s_wt, s_m, s_mc = signal("s_wt"), signal("s_m"), signal("s_m_copied")
        s_all = signal("s_all_reduced")
        n_step = [0]

        def step(fn, key=None):
            settled("dve")
            n_step[0] += 1
            do("dve", fn, s_w, n_step[0])
            if key:
                s_w.at[key] = s_w.count

        def settled(engine):
            if n_step[0]:
                wait(engine, s_w, n_step[0])

        def largest_of(dst, src, key):
            do("dve", lambda e: e.tensor_reduce(dst, src, AX.X, ALU.max, apply_absolute_value=True), s_w, key)

        def over_partitions(cols, key):
            wait("pool", s_w, key)
            do("pool", lambda e: e.partition_all_reduce(largest[:, cols], part[:, cols], P, ROP.max), s_all, key)

        def inverses(cols, key):
            wait("dve", s_all, key)
            step(lambda e: e.tensor_scalar(largest[:, cols], largest[:, cols], TINY, None, ALU.max))
            step(lambda e: e.reciprocal(inv[:, cols], largest[:, cols]))

        def high(src32, hi, key, scale=1.0):
            settled("act")
            if isinstance(scale, float):
                do("act", lambda e: e.activation(hi, src32, ACT.Copy), s_hi, key)
            else:
                do("act", lambda e: e.activation(hi, src32, ACT.Identity, scale=scale), s_hi, key)

        def low(src32, hi, lo, key, scale=None):
            wait("dve", s_hi, key)
            settled("dve")
            if scale is None:
                do("dve", lambda e: e.tensor_tensor(lo, src32, hi, ALU.subtract), s_w, key)
            else:
                do("dve", lambda e: e.scalar_tensor_tensor(lo, src32, scale, hi, ALU.mult, ALU.subtract), s_w, key)

        t_banks, m_banks = {(0, 0): bank[0], (0, 1): bank[1], (1, 0): bank[2], (1, 1): bank[4]}, bank[5:7] + bank[0:2]
        wait("pe", s_id, "ident")
        wait("pe", qk_loaded, "w")
        for j in range(2):
            for i in range(2):
                ps = t_banks[j, i]
                for c in range(4):
                    do("pe", lambda e, ps=ps, c=c, i=i, j=j: e.transpose(
                        ps[:, c * P:(c + 1) * P], W[:, i, (4 * j + c) * P:(4 * j + c + 1) * P], ident[:, :]),
                        *((s_wt, (j, i)) if c == 3 else ()))
                wait("dve", s_wt, (j, i))
                for c in range(4):
                    do("dve", lambda e, ps=ps, c=c, i=i, j=j: e.tensor_scalar(
                        WT[:, i, 4 * j + c, :], ps[:, c * P:(c + 1) * P], ps[:, c * P + D - 1:c * P + D], None,
                        ALU.subtract), *((s_w, ("WT", j, i)) if c == 3 else ()))
        M_by_pair = M32.rearrange("p (c hh) d -> p c hh d", hh=2)
        for j in range(2):
            wait("pe", s_w, ("WT", j, 1))
            for odd in range(2):
                ps, rows = m_banks[2 * j + odd], slice(odd * E, (odd + 1) * E)
                for c in range(4):
                    do("pe", lambda e, ps=ps, c=c, j=j, rows=rows: e.matmul(
                        ps[:, c * D:(c + 1) * D], WT[rows, 0, 4 * j + c, :], WT[rows, 1, 4 * j + c, :], start=True, stop=True),
                        *((s_m, (j, odd)) if c == 3 else ()))
                wait("act", s_m, (j, odd))
                do("act", lambda e, ps=ps, j=j, odd=odd: e.activation(
                    M_by_pair[:, 4 * j:4 * j + 4, odd, :], ps[:, :].rearrange("p (c d) -> p c d", c=4), ACT.Copy),
                    s_mc, (j, odd))

        heads_of = lambda j: slice(8 * j, 8 * j + 8)

        def m_largest(j):
            wait("dve", s_mc, (j, 1))
            largest_of(part[:, heads_of(j)], M32[:, heads_of(j), :], ("part", j))
            over_partitions(heads_of(j), ("part", j))

        def m_scaled(j):
            hs = heads_of(j)
            inverses(hs, ("part", j))
            do("dve", lambda e: e.tensor_scalar(s_exp[:, hs], largest[:, hs], float(E) ** -0.5, None, ALU.mult))
            step(lambda e: e.tensor_tensor(M32[:, hs, :], M32[:, hs, :],
                                           inv[:, hs].unsqueeze(2).to_broadcast([P, 8, D]), ALU.mult))
            high(M32[:, hs, :], Mh[:, hs, :], ("M", j))

        def m_low(j):
            low(M32[:, heads_of(j), :], Mh[:, heads_of(j), :], Ml[:, heads_of(j), :], ("M", j))

        def v_less_last():
            wait("pool", v_loaded, "w")
            do("pool", lambda e: e.tensor_tensor(W[:, 2, :], W[:, 2, :], Wv_last[:, :], ALU.subtract), s_all, "Wv")

        def v_largest():
            wait("dve", s_all, "Wv")
            largest_of(part[:, 16:17], W[:, 2, :], "part_v")
            over_partitions(slice(16, 17), "part_v")

        def v_high():
            inverses(slice(16, 17), "part_v")
            high(W[:, 2, :], Wvh[:, :], "Wv", inv[:, 16:17])

        def v_low():
            low(W[:, 2, :], Wvh[:, :], Wvl[:, :], "Wv", inv[:, 16:17])

        def p_largest():
            wait("dve", wp_loaded, "wp")
            largest_of(part[:, 17:18], Wp[:, :, :].rearrange("p c o -> p (c o)"), "part_p")
            over_partitions(slice(17, 18), "part_p")

        def p_high():
            inverses(slice(17, 18), "part_p")
            do("dve", lambda e: e.tensor_tensor(s_y[:, :], largest[:, 16:17], largest[:, 17:18], ALU.mult))
            high(Wp[:, :, :], Wph[:, :, :], "Wp", inv[:, 17:18])

        def p_low():
            low(Wp[:, :, :], Wph[:, :, :], Wpl[:, :, :], "Wp", inv[:, 17:18])

        s_ft, s_fb = signal("s_ffn_t"), signal("s_ffn_bias")
        held_bank = [None]

        def sum_w1():
            wait("dve", ffn_loaded, "ffn")
            do("dve", lambda e: e.tensor_reduce(psums[:, 0:1], w1[:, :, :].rearrange("p c d -> p (c d)"), AX.X, ALU.add,
                                                apply_absolute_value=True))

        def sum_w2():
            do("dve", lambda e: e.tensor_reduce(psums[:, 1:2], w2[:, :], AX.X, ALU.add, apply_absolute_value=True),
               s_w, "psums")
            wait("pool", s_w, "psums")
            do("pool", lambda e: e.partition_all_reduce(sums[:, :], psums[:, :], P, ROP.add), s_all, "sums")
            do("dve", lambda e: e.tensor_reduce(part[:, 18:19], g1[:, :], AX.X, ALU.max, apply_absolute_value=True))
            largest_of(part[:, 19:20], g2[:, :], "part_g")
            over_partitions(slice(18, 20), "part_g")

        def w_scales():
            inverses(slice(18, 20), "part_g")
            wait("dve", s_all, "sums")
            step(lambda e: e.tensor_scalar(clip[:, :], sums[:, :], 1.0 / (F * D), 1e-5, ALU.mult, ALU.max))
            step(lambda e: e.reciprocal(sc[:, :], clip[:, :]))

        def f_scales():
            step(lambda e: e.reciprocal(rsc[:, :], sc[:, :]))
            do("dve", lambda e: e.tensor_scalar(gs1[:, :], g1[:, :], inv[:, 18:19], None, ALU.mult))
            do("dve", lambda e: e.tensor_scalar(gs2[:, :], g2[:, :], inv[:, 19:20], None, ALU.mult))
            step(lambda e: e.tensor_tensor(s_f1[:, :], rsc[:, 0:1], largest[:, 18:19], ALU.mult))
            step(lambda e: e.tensor_tensor(s_f2[:, :], rsc[:, 1:2], largest[:, 19:20], ALU.mult))

        def ternary(i):
            m = misc_take()
            wait("pe", ffn_loaded, "ffn")
            for c in range(FC):
                src = w1[:, c, :] if i == 0 else w2[:, c * P:(c + 1) * P]
                do("pe", lambda e, c=c, src=src: e.transpose(m[:, c * P:(c + 1) * P], src, ident[:, :]),
                   *((s_ft, i) if c == FC - 1 else ()))
            misc_read(s_w, ("ternary", i))

            def compare():
                wait("dve", s_ft, i)
                settled("dve")
                do("dve", lambda e: e.tensor_scalar(above[i][:, :], m[:, :], sc[:, i:i + 1], 0.5, ALU.mult, ALU.is_gt))
                step(lambda e: e.tensor_scalar(below[i][:, :], m[:, :], sc[:, i:i + 1], -0.5, ALU.mult, ALU.is_lt),
                     ("ternary", i))
            later.append(compare)

        def ternary_out(i):
            step(lambda e: e.tensor_tensor(tern[i][:, :], above[i][:, :], below[i][:, :], ALU.subtract))

        def gains(i):
            if i == 0:
                step(lambda e: e.tensor_scalar(above[0][:, :], tern[0][:, :], gs1[:, :], None, ALU.mult))
                hi, lo = T1h[:, :], T1l[:, :]
            else:
                settled("dve")
                for c in range(FC):
                    fn = (lambda e, c=c: e.tensor_scalar(above[1][:, c * D:(c + 1) * D], tern[1][:, c * D:(c + 1) * D],
                                                         gs2[:, c:c + 1], None, ALU.mult))
                    step(fn) if c == FC - 1 else do("dve", fn)
                hi, lo = (T[:, :, :].rearrange("p c d -> p (c d)") for T in (T2h, T2l))
            high(above[i][:, :], hi, f"T{i}")
            later.append(lambda: low(above[i][:, :], hi, lo, f"T{i}"))

        def bias1_product():
            step(lambda e: e.tensor_scalar(lbrep1[:, :], ones[:, :], lb1[:, :], None, ALU.mult))
            m = misc_take()
            settled("pe")
            do("pe", lambda e: e.matmul(m[:, :], lbrep1[:, :], tern[0][:, :], start=True, stop=True), s_fb, 0)
            misc_read(s_w, "bias1")

            def add():
                wait("dve", s_fb, 0)
                wait("dve", rows_loaded, "rows")
                step(lambda e: e.reciprocal(inv_f1[:, :], s_f1[:, :]))
                step(lambda e: e.scalar_tensor_tensor(bn[:, :], m[:, :], rsc[:, 0:1], b1_all[:, :], ALU.mult, ALU.add), "bias1")
            later.append(add)

        def bias1_scaled():
            step(lambda e: e.tensor_scalar(bn[:, :], bn[:, :], inv_f1[:, :], None, ALU.mult))

        def bias1_part(i):
            step(lambda e: e.tensor_copy(bpart[i][:, :], bn[:, :]))
            if i < 2:
                step(lambda e: e.tensor_tensor(bn[:, :], bn[:, :], bpart[i][:, :], ALU.subtract))
            settled("dve")
            do("dve", lambda e: e.tensor_copy(bias_rows[32 * i:32 * i + 1, :], bpart[i][32 * i:32 * i + 1, :]),
               s_w, f"bias{i}")

        def bias2_product():
            settled("dve")
            for c in range(FC):
                fn = lambda e, c=c: e.tensor_scalar(lbrep2[:, c, :], ones[:, :], lb2[:, c:c + 1], None, ALU.mult)
                step(fn) if c == FC - 1 else do("dve", fn)
            m = misc_take()
            settled("pe")
            for c in range(FC):
                do("pe", lambda e, c=c: e.matmul(m[:, 0:D], lbrep2[:, c, :], tern[1][:, c * D:(c + 1) * D],
                                                 start=c == 0, stop=c == FC - 1), *((s_fb, 1) if c == FC - 1 else ()))
            misc_read(s_w, "ffn_weights")

            def add():
                wait("dve", s_fb, 1)
                do("dve", lambda e: e.scalar_tensor_tensor(bias2[:, :], m[:, 0:D], rsc[:, 1:2], b2_all[:, :],
                                                           ALU.mult, ALU.add), s_w, "ffn_weights")
            later.append(add)

        pieces = [sum_w1, sum_w2, w_scales, f_scales]
        for i in range(2):
            pieces += [lambda i=i: ternary(i), lambda i=i: ternary_out(i), lambda i=i: gains(i)]
        pieces += [bias1_product, bias1_scaled] + [lambda i=i: bias1_part(i) for i in range(3)] + [bias2_product]
        work_at = {(b, s): [] for b in range(-2, B + 1) for s in range(H)}
        for n, fn in enumerate(pieces):
            work_at[1 + n // len(PIECE_STEPS), PIECE_STEPS[n % len(PIECE_STEPS)]].append(fn)
        for g, fn in ((0, lambda: m_scaled(1)), (1, v_largest), (2, lambda: m_low(1)), (4, v_high), (5, v_low),
                      (12, p_largest), (14, p_high), (17, p_low)):
            work_at[divmod(g - Q_LEAD, H)].append(fn)

        s_st, s_r0, s_xn, s_xbp = signal("s_ln_stats"), signal("s_ln_root"), signal("s_xn"), signal("s_x_plus_bp")
        s_misc = signal("s_misc_ready")
        s_mhi, s_mlo = signal("s_misc_hi"), signal("s_misc_lo")
        s_q, s_qhi, s_qlo = signal("s_q"), signal("s_q_hi"), signal("s_q_lo")
        s_ms, s_mx = signal("s_max_scores"), signal("s_max")
        s_sh = [signal(f"s_shift{i}", 16) for i in range(2)]
        s_sc, s_exp_done, s_ph, s_pl = signal("s_scores"), signal("s_exp"), signal("s_p_hi"), signal("s_p_lo")
        s_pv, s_o1, s_o, s_on = signal("s_pv"), signal("s_o_part"), signal("s_o"), signal("s_o_normal")
        s_x1 = signal("s_x1_stats")
        sc_bank, pv_bank, misc_banks = bank[0:2], bank[4:6], (bank[3], bank[7])
        ms_bank = lambda g: bank[5] if g < MAX_LEAD and g % 2 else bank[2]
        q_bank = lambda g: bank[4] if g < Q_LEAD and g // 2 % 2 else bank[6]
        ms_last, q_last = {}, {}
        misc_reader, misc_turn = [None, None], [0]

        def misc_take():
            misc_turn[0] ^= 1
            if misc_reader[misc_turn[0]]:
                wait("pe", *misc_reader[misc_turn[0]])
            return misc_banks[misc_turn[0]]

        def misc_read(sig, key):
            misc_reader[misc_turn[0]] = (sig, key)

        later = []

        def norm_stats(b):
            wait("dve", x_of[b], "x")
            if b:
                wait("dve", s_r0, b - 1)
            for t in range(NB):
                do("dve", lambda e, t=t: e.bn_stats(st0[:, t, :], X[:, NB * b + t, :]), s_st, ("st", b))
            wait("dve", s_st, ("st", b))
            for t in range(NB):
                do("dve", lambda e, t=t: e.bn_aggr(mv0[:, t, :], st0[:, t, :]), s_st, ("mv", b))

        def norm_root(b):
            wait("pool", s_st, ("mv", b))
            wait("pool", s_const, "half")
            do("pool", lambda e: e.tensor_scalar(ve0[:, :], mv0[:, :, 1], EPS, None, ALU.add), s_r0, ("ve", b))
            wait("pool", s_r0, ("ve", b))
            if b:
                wait("pool", s_xn, b - 1)
            do("pool", lambda e: e.tensor_tensor(r0[:, :], ve0[:, :], half[:, :], ALU.pow), s_r0, b)

        def norm_apply(b):
            wait("dve", s_r0, b)
            wait("dve", s_st, ("mv", b))
            if b:
                wait("dve", s_misc, ("xT", b - 1))
            for t in range(NB):
                do("dve", lambda e, t=t: e.tensor_scalar(xn[:, t, 0:D - 1], X[:, NB * b + t, 0:D - 1], mv0[:, t, 0:1],
                                                         r0[:, t:t + 1], ALU.subtract, ALU.mult), s_xn, b)

        def add_bp(b):
            wait("pool", s_xn, b)
            wait("pool", bp_loaded, "bp")
            tiles = X[:, NB * b:NB * b + NB, :]
            do("pool", lambda e: e.tensor_tensor(tiles, tiles, bp_all[:, :].unsqueeze(1).to_broadcast([P, NB, D]), ALU.add),
               s_xbp, b)

        def low_part(lo, src, hi, key):
            def fn():
                wait("dve", s_mhi, key)
                do("dve", lambda e: e.tensor_tensor(lo, src, hi, ALU.subtract), s_mlo, key)
            misc_read(s_mlo, key)
            later.append(fn)

        def x_transposed(b):
            r = b % XT_RING
            misc = misc_take()
            wait("pe", s_xn, b)
            wait("pe", s_dc, "consts")
            for t in range(NB):
                do("pe", lambda e, t=t: e.transpose(misc[:, t * P:(t + 1) * P], xn[:, t, :], ident[:, :]),
                   *((s_misc, ("xT", b)) if t == NB - 1 else ()))
            wait("act", s_misc, ("xT", b))
            if b >= XT_RING:
                wait("act", s_sc, H * (b - XT_RING) + H - 1)
            do("act", lambda e: e.activation(xTh[r][:, :], misc[:, 0:N], ACT.Copy), s_mhi, ("xT", b))
            low_part(xTl[r][:, :], misc[:, 0:N], xTh[r][:, :], ("xT", b))

        def queries(g):
            b, h, r = g // H, g % H, (g // H) % XT_RING
            wait("pe", s_mlo, ("xT", b))
            wait("pe", s_w, ("M", h // 8))
            dst = q_bank(g)
            if id(dst) in q_last:
                wait("pe", s_qlo, q_last[id(dst)])
            q_last[id(dst)] = g
            for j in range(2):
                o = dst[:, j * N:(j + 1) * N]
                for n, (m, xt) in enumerate(((Mh, xTh), (Mh, xTl), (Ml, xTh))):
                    do("pe", lambda e, o=o, m=m, xt=xt, j=j, n=n: e.matmul(
                        o, m[:, h + j, :], xt[r][:, :], start=n == 0, stop=n == 2),
                        *((s_q, g) if (j, n) == (1, 2) else ()))

        def queries_out(g):
            b, h = g // H, g % H
            wait("act", s_q, g)
            if b >= 2:
                wait("act", s_sc, g + 1 - 2 * H)
            src = q_bank(g)[:, :].rearrange("p (j n) -> p j n", j=2)
            hi, lo = Qh[b % 2][:, h:h + 2, :], Ql[b % 2][:, h:h + 2, :]
            do("act", lambda e: e.activation(hi, src, ACT.Copy), s_qhi, g)

            def q_low():
                wait("dve", s_qhi, g)
                do("dve", lambda e: e.tensor_tensor(lo, src, hi, ALU.subtract), s_qlo, g)
            later.append(q_low)

        def max_scores(g):
            b, h = g // H, g % H
            wait("pe", s_qhi, g - g % 2)
            dst = ms_bank(g)
            if id(dst) in ms_last:
                wait("pe", s_mx, ms_last[id(dst)])
            ms_last[id(dst)] = g
            for t in range(NB):
                do("pe", lambda e, t=t: e.matmul(dst[:, t * N:(t + 1) * N], Qh[b % 2][:, h, t * P:(t + 1) * P],
                                                 xTh[b % XT_RING][:, :], start=True, stop=True),
                   *((s_ms, g) if t == NB - 1 else ()))

        def max_out(g):
            b, h = g // H, g % H
            wait("dve", s_ms, g)
            if b >= 2:
                wait("dve", s_misc, ("shift", b - 2))
            do("dve", lambda e: e.tensor_reduce(negmax[b % 2][:, NB * h:NB * h + NB],
                                                ms_bank(g)[:, :].rearrange("p (t m) -> p t m", t=NB),
                                                AX.X, ALU.max, negate=True), s_mx, g)

        def shift_rows(b):
            misc = misc_take()
            wait("pe", s_mx, H * b + H - 1)
            do("pe", lambda e: e.transpose(misc[:, 0:P], negmax[b % 2][:, :], ident[:, :]), s_misc, ("shift", b))
            misc_read(s_mlo, ("shift", b))

            def out_and_over():
                wait("dve", s_misc, ("shift", b))
                if b >= 2:
                    wait("dve", s_sh[b % 2], b - 2)
                do("dve", lambda e: e.tensor_copy(shift[b % 2][:, :], misc[0:H * NB, 0:P]), s_mlo, ("shift", b))
                wait("sp", s_mlo, ("shift", b))
                wait("sp", s_qlo, H * b + H - 2)
                do("sp", lambda e: e.dma_start(Qh[b % 2][D - 1:D, :, :].rearrange("p h (t n) -> p (h t) n", t=NB),
                                               shift[b % 2][:, :]), s_sh[b % 2], b)
            later.append(out_and_over)

        def scores(g):
            b, h, r = g // H, g % H, (g // H) % XT_RING
            wait("pe", s_sh[b % 2], b)
            wait("pe", s_qlo, g - g % 2)
            if g >= 2:
                wait("pe", s_exp_done, g - 2)
            for t in range(NB):
                o = sc_bank[g % 2][:, t * N:(t + 1) * N]
                for n, (xt, qq) in enumerate(((xTh, Qh), (xTh, Ql), (xTl, Qh))):
                    do("pe", lambda e, o=o, xt=xt, qq=qq, t=t, n=n: e.matmul(
                        o, xt[r][:, t * P:(t + 1) * P], qq[b % 2][:, h, :], start=n == 0, stop=n == 2),
                        *((s_sc, g) if (t, n) == (NB - 1, 2) else ()))

        def exps(g):
            i = g % P_RING
            wait("act", s_sc, g)
            if g >= P_RING:
                wait("act", s_pl, g - P_RING)
                wait("act", s_ph, g - P_RING)
            do("act", lambda e: e.activation(p32[i][:, :, :], sc_bank[g % 2][:, :].rearrange("p (t n) -> p t n", t=NB),
                                             ACT.Exp, scale=s_exp[:, g % H:g % H + 1]), s_exp_done, g)

        def split_p(g):
            i = g % P_RING
            wait("act", s_exp_done, g)
            if g >= P_RING:
                wait("act", s_pv, g - P_RING)
                wait("pool", s_pv, g - P_RING)
            do("act", lambda e: e.activation(ph[i][:, :, :], p32[i][:, :, :], ACT.Copy), s_ph, g)
            wait("pool", s_ph, g)
            do("pool", lambda e: e.tensor_tensor(pl[i][:, :, :], p32[i][:, :, :], ph[i][:, :, :], ALU.subtract), s_pl, g)

        def values(b, m, half_):
            r, cols = b % XT_RING, slice(half_ * 512, half_ * 512 + 512)
            h0 = half_ * 8
            misc = misc_take()
            wait("pe", s_mlo, ("xT", b))
            wait("pe", s_w, "Wv")
            for n, (xt, w) in enumerate(((xTh, Wvh), (xTh, Wvl), (xTl, Wvh))):
                do("pe", lambda e, xt=xt, w=w, n=n: e.matmul(misc[:, :], xt[r][:, m * P:(m + 1) * P], w[:, cols],
                                                             start=n == 0, stop=n == 2),
                   *((s_misc, ("V", b, m, half_)) if n == 2 else ()))
            key = ("V", b, m, half_)
            src = misc[:, :].rearrange("p (h e) -> p h e", h=8)
            hi, lo = V[b % 2][:, m, h0:h0 + 8, E:2 * E], V[b % 2][:, m, h0:h0 + 8, 0:E]
            wait("act", s_misc, key)
            if b >= 2:
                wait("act", s_pv, H * (b - 2) + H - 1)
            do("act", lambda e: e.activation(hi, src, ACT.Copy), s_mhi, key)
            low_part(lo, src, hi, key)

        def weighted(g):
            b, h, i = g // H, g % H, g % P_RING
            wait("pe", s_pl, g)
            for m in range(NB):
                wait("pe", s_mlo, ("V", b, m, h // 8))
            if g >= 2:
                wait("pe", s_o, g - 2)
            elif id(pv_bank[g]) in q_last:
                wait("pe", s_qlo, q_last[id(pv_bank[g])])
            elif id(pv_bank[g]) in ms_last:
                wait("pe", s_mx, ms_last[id(pv_bank[g])])
            for t in range(NB):
                for m in range(NB):
                    for pp, lo in ((ph, 0), (pl, E)):
                        do("pe", lambda e, t=t, m=m, pp=pp, lo=lo: e.matmul(
                            pv_bank[g % 2][:, t * N + lo:t * N + 2 * E + 1], pp[i][:, m, t * P:(t + 1) * P],
                            V[b % 2][:, m, h, lo:2 * E + 1], start=m == 0 and lo == 0, stop=m == NB - 1 and lo == E),
                            *((s_pv, g) if (t, m, lo) == (NB - 1, NB - 1, E) else ()))

        def weighted_out(g):
            b, h = g // H, g % H
            src = pv_bank[g % 2][:, :].rearrange("p (t n) -> p t n", t=NB)
            wait("act", s_pv, g)
            if g >= 2:
                wait("act", s_o, g - 2)
            do("act", lambda e: e.activation(o_part[g % 2][:, :, :], src[:, :, E:2 * E], ACT.Copy), s_o1, g)

            def add():
                wait("dve", s_o1, g)
                if b >= 2:
                    wait("dve", s_misc, ("OT", b - 2, h // GH))
                    wait("dve", s_on, (b - 2, h // GH))
                do("dve", lambda e: e.reciprocal(rsum[b % 2][:, :, h], src[:, :, 2 * E]))
                do("dve", lambda e: e.tensor_tensor(O[b % 2][:, :, h, :], src[:, :, 0:E], o_part[g % 2][:, :, :], ALU.add),
                   s_o, g)
            later.append(add)

        def normalise(b, k):
            h0 = GH * k
            wait("pool", s_o, H * b + h0 + GH - 1)
            tile = O[b % 2][:, :, h0:h0 + GH, :]
            do("pool", lambda e: e.tensor_tensor(tile, tile, rsum[b % 2][:, :, h0:h0 + GH].unsqueeze(3)
                                                 .to_broadcast([P, NB, GH, E]), ALU.mult), s_on, (b, k))

        def outputs_transposed(b, k):
            misc = misc_take()
            wait("pe", s_on, (b, k))
            key = ("OT", b, k)
            for cc in range(2):
                for t in range(NB):
                    h0 = GH * k + 2 * cc
                    do("pe", lambda e, cc=cc, t=t, h0=h0: e.transpose(
                        misc[:, (cc * NB + t) * P:(cc * NB + t + 1) * P],
                        O[b % 2][:, t, h0:h0 + 2, :].rearrange("p h e -> p (h e)"), ident[:, :]),
                        *((s_misc, key) if (cc, t) == (1, NB - 1) else ()))
            src = misc[:, :].rearrange("p (c n) -> p c n", c=2)
            hi, lo = OTh[:, 2 * k:2 * k + 2, :], OTl[:, 2 * k:2 * k + 2, :]
            wait("act", s_misc, key)
            if b:
                wait("act", s_misc, ("y", b - 1))
            do("act", lambda e: e.activation(hi, src, ACT.Copy), s_mhi, key)
            low_part(lo, src, hi, key)

        y_bank = [None]

        def project(b, t):
            if t == 0:
                y_bank[0] = misc_take()
                wait("pe", s_mlo, ("OT", b, H // GH - 1))
                wait("pe", s_w, "Wp")
            misc = y_bank[0]
            for c in range(HC):
                for n, (o, w) in enumerate(((OTh, Wph), (OTh, Wpl), (OTl, Wph))):
                    do("pe", lambda e, c=c, n=n, o=o, w=w: e.matmul(
                        misc[:, t * D:(t + 1) * D], o[:, c, t * P:(t + 1) * P], w[:, c, :],
                        start=(c, n) == (0, 0), stop=(c, n) == (HC - 1, 2)),
                        *((s_misc, ("y", b)) if (t, c, n) == (NB - 1, HC - 1, 2) else ()))

        def residual(b):
            misc = y_bank[0]
            tiles = X[:, NB * b:NB * b + NB, :]

            def add():
                wait("dve", s_misc, ("y", b))
                wait("dve", s_xbp, b)
                do("dve", lambda e: e.scalar_tensor_tensor(tiles, misc[:, 0:NB * D].rearrange("p (t d) -> p t d", t=NB),
                                                           s_y[:, :], tiles, ALU.mult, ALU.add), s_mlo, ("y", b))
            later.append(add)
            misc_reader[misc_banks.index(misc)] = (s_mlo, ("y", b))

        def ffn_stats(b):
            wait("dve", s_mlo, ("y", b))
            for t in range(NB):
                do("dve", lambda e, t=t: e.bn_stats(st1[:, t, :], X[:, NB * b + t, :]), s_x1, ("st", b))
            wait("dve", s_x1, ("st", b))
            for t in range(NB):
                do("dve", lambda e, t=t: e.bn_aggr(mv1[:, NB * b + t, :], st1[:, t, :]), s_x1, ("mv", b))

        s_r1 = signal("s_ffn_root")

        def ffn_root(b):
            tl = slice(NB * b, NB * b + NB)
            wait("pool", s_x1, ("mv", b))
            do("pool", lambda e: e.tensor_scalar(ve1[:, tl], mv1[:, tl, 1], 1.0 + EPS, EPS * EPS, ALU.mult, ALU.add),
               s_r1, ("ve", b))
            wait("pool", s_r1, ("ve", b))
            do("pool", lambda e: e.tensor_tensor(r1[:, tl], ve1[:, tl], half[:, :], ALU.pow), s_r1, b)

        def batch_work(b, s):
            ok = lambda c: 0 <= c < B
            if s == 2 and ok(b + 2) and b >= -1:
                norm_stats(b + 2)
                norm_root(b + 2)
            if s == 4 and ok(b + 2) and b >= -1:
                norm_apply(b + 2)
                add_bp(b + 2)
            if s == 6 and ok(b + 2) and b >= -1:
                x_transposed(b + 2)
            if s in VALUE_STEPS and ok(b + 1):
                n = VALUE_STEPS.index(s)
                values(b + 1, n % 2, n // 2)
            if s == 13 and ok(b + 1):
                shift_rows(b + 1)
            for k, (at, back) in enumerate(((7, 0), (11, 0), (15, 0), (3, 1))):
                if s == at and ok(b - back):
                    normalise(b - back, k)
            if s in (8, 9) and ok(b - 1):
                project(b - 1, s - 8)
            if s == 9 and ok(b - 1):
                residual(b - 1)
            for k, (at, back) in enumerate(((9, 0), (13, 0), (1, 1), (5, 1))):
                if s == at and ok(b - back):
                    outputs_transposed(b - back, k)
            for fn in work_at[b, s]:
                fn()
            if s == 11 and ok(b - 1):
                ffn_stats(b - 1)
                ffn_root(b - 1)

        live = lambda g: 0 <= g < NH
        norm_stats(0)
        norm_root(0)
        m_largest(0)
        norm_apply(0)
        add_bp(0)
        x_transposed(0)
        m_scaled(0)
        m_largest(1)
        v_less_last()
        later.pop()()
        m_low(0)
        for t in range(-2 * H + 4, NH + H - 2):
            held, later[:] = list(later), []
            if live(t - 1 + MAX_LEAD):
                max_out(t - 1 + MAX_LEAD)
            for fn in held:
                fn()
            if live(t):
                scores(t)
                exps(t)
            if live(t - PV_LAG):
                weighted(t - PV_LAG)
                weighted_out(t - PV_LAG)
            if live(t):
                split_p(t)
            if live(t + MAX_LEAD):
                max_scores(t + MAX_LEAD)
            if t % 2 == 0 and live(t + Q_LEAD):
                queries(t + Q_LEAD)
                queries_out(t + Q_LEAD)
            batch_work(t // H, t % H)
        setup.close()

        L_YT, L_YLO, L_HID, L_STAT, L_NORM, L_ZT, L_ZLO, L_OUT, L_SUM = 1, 2, 3, 4, 5, 6, 7, 8, 9
        A_RING = 4
        y = [sb(f"y{i}", [P, D]) for i in range(2)]
        yTh = [sb(f"yTh{i}", [P, P], F16) for i in range(3)]
        yTl = [sb(f"yTl{i}", [P, P], F16) for i in range(3)]
        a = [sb(f"a{i}", [P, F]) for i in range(A_RING)]
        z = [sb(f"z{i}", [P, F]) for i in range(2)]
        zTh = [sb(f"zTh{i}", [P, FC, P], F16) for i in range(3)]
        zTl = [sb(f"zTl{i}", [P, FC, P], F16) for i in range(3)]
        st2 = [sb(f"st2_{i}", [P, 6]) for i in range(2)]
        mv2 = [sb(f"mv2_{i}", [P, 2]) for i in range(A_RING)]
        ve2 = [sb(f"ve2_{i}", [P, 1]) for i in range(A_RING)]
        r2 = [sb(f"r2_{i}", [P, 1]) for i in range(A_RING)]
        nm2 = [sb(f"nm2_{i}", [P, 1]) for i in range(A_RING)]
        s_y1, s_yt, s_yhi, s_ylo = signal("s_ffn_y"), signal("s_ffn_yT"), signal("s_ffn_y_hi"), signal("s_ffn_y_lo")
        s_pre, s_a, s_st2, s_r2, s_nm2 = (signal(f"s_ffn_{n}") for n in ("pre", "gelu", "stats2", "root2", "negmean"))
        s_z, s_zt, s_zhi, s_zlo = (signal(f"s_ffn_{n}") for n in ("z", "zT", "z_hi", "z_lo"))
        s_xb, s_f, s_out = signal("s_ffn_x_plus_bias"), signal("s_ffn_out"), signal("s_ffn_sum")
        s_store = signal("s_store", 16)
        yT_bank, pre_bank, z_bank, f_bank = bank[0:2], bank[2:4], bank[4:6], bank[6:8]
        STORE = 4
        out_tok = out.rearrange("b (t p) d -> p (b t) d", p=P)

        def free(engine, sig, i, ring):
            if i >= ring:
                wait(engine, sig, i - ring)

        def f_y(i):
            wait("dve", s_r1, i // NB)
            free("dve", s_yt, i, 2)
            do("dve", lambda e: e.tensor_scalar(y[i % 2][:, :], X[:, i, :], mv1[:, i, 0:1], r1[:, i:i + 1],
                                                ALU.subtract, ALU.mult), s_y1, i)

        def f_bias(i):
            wait("pool", s_y1, i)
            do("pool", lambda e: e.tensor_tensor(X[:, i, :], X[:, i, :], bias2[:, :], ALU.add), s_xb, i)

        def f_yT(i):
            wait("pe", s_y1, i)
            free("pe", s_ylo, i, 2)
            do("pe", lambda e: e.transpose(yT_bank[i % 2][:, 0:P], y[i % 2][:, :], ident[:, :]), s_yt, i)

        def f_yhi(i):
            wait("act", s_yt, i)
            free("act", s_pre, i, 3)
            do("act", lambda e: e.activation(yTh[i % 3][:, :], yT_bank[i % 2][:, 0:P], ACT.Copy), s_yhi, i)

        def f_ylo(i):
            wait("dve", s_yhi, i)
            free("dve", s_pre, i, 3)
            do("dve", lambda e: e.tensor_tensor(yTl[i % 3][:, :], yT_bank[i % 2][:, 0:P], yTh[i % 3][:, :], ALU.subtract),
               s_ylo, i)

        def f_hidden(i):
            wait("pe", s_ylo, i)
            free("pe", s_a, i, 2)
            o = pre_bank[i % 2][:, :]
            do("pe", lambda e: e.matmul(o, ones_bf[:, :], bias_rows[:, :], start=True, stop=False))
            do("pe", lambda e: e.matmul(o, yTh[i % 3][:, :], T1h[:, :], start=False, stop=False))
            do("pe", lambda e: e.matmul(o, yTh[i % 3][:, :], T1l[:, :], start=False, stop=False))
            do("pe", lambda e: e.matmul(o, yTl[i % 3][:, :], T1h[:, :], start=False, stop=True), s_pre, i)

        def f_gelu(i):
            wait("act", s_pre, i)
            free("act", s_z, i, A_RING)
            free("act", s_st2, i, A_RING)
            do("act", lambda e: e.activation(a[i % A_RING][:, :], pre_bank[i % 2][:, :], ACT.Gelu, scale=s_f1[:, :]), s_a, i)

        def f_stats(i):
            k = i % A_RING
            wait("dve", s_a, i)
            free("dve", s_st2, i, 2)
            do("dve", lambda e: e.bn_stats(st2[i % 2][:, :], a[k][:, :]), s_st2, ("st", i))
            wait("dve", s_st2, ("st", i))
            free("dve", s_r2, i, A_RING)
            free("dve", s_nm2, i, A_RING)
            do("dve", lambda e: e.bn_aggr(mv2[k][:, :], st2[i % 2][:, :]), s_st2, i)

        def f_root(i):
            k = i % A_RING
            wait("pool", s_st2, i)
            do("pool", lambda e: e.tensor_scalar(ve2[k][:, :], mv2[k][:, 1:2], EPS, None, ALU.add), s_r2, ("ve", i))
            wait("pool", s_r2, ("ve", i))
            free("pool", s_z, i, A_RING)
            free("pool", s_nm2, i, A_RING)
            do("pool", lambda e: e.tensor_tensor(r2[k][:, :], ve2[k][:, :], half[:, 0:1], ALU.pow), s_r2, i)

        def f_negmean(i):
            k = i % A_RING
            wait("dve", s_r2, i)
            free("dve", s_z, i, A_RING)
            do("dve", lambda e: e.scalar_tensor_tensor(nm2[k][:, :], mv2[k][:, 0:1], -1.0, r2[k][:, :], ALU.mult, ALU.mult),
               s_nm2, i)

        def f_norm(i):
            k = i % A_RING
            wait("act", s_nm2, i)
            free("act", s_zt, i, 2)
            do("act", lambda e: e.activation(z[i % 2][:, :], a[k][:, :], ACT.Identity, scale=r2[k][:, :], bias=nm2[k][:, :]),
               s_z, i)

        def f_zT(i):
            wait("pe", s_z, i)
            free("pe", s_zlo, i, 2)
            for c in range(FC):
                do("pe", lambda e, c=c: e.transpose(z_bank[i % 2][:, c * P:(c + 1) * P], z[i % 2][:, c * P:(c + 1) * P],
                                                    ident[:, :]), *((s_zt, i) if c == FC - 1 else ()))

        z_ps = lambda i: z_bank[i % 2][:, :].rearrange("p (c n) -> p c n", c=FC)

        def f_zhi(i):
            wait("act", s_zt, i)
            free("act", s_f, i, 3)
            do("act", lambda e: e.activation(zTh[i % 3][:, :, :], z_ps(i), ACT.Copy), s_zhi, i)

        def f_zlo(i):
            wait("dve", s_zhi, i)
            free("dve", s_f, i, 3)
            do("dve", lambda e: e.tensor_tensor(zTl[i % 3][:, :, :], z_ps(i), zTh[i % 3][:, :, :], ALU.subtract), s_zlo, i)

        def f_out(i):
            wait("pe", s_zlo, i)
            free("pe", s_out, i, 2)
            for c in range(FC):
                for n, (zz, w) in enumerate(((zTh, T2h), (zTh, T2l), (zTl, T2h))):
                    do("pe", lambda e, c=c, n=n, zz=zz, w=w: e.matmul(
                        f_bank[i % 2][:, 0:D], zz[i % 3][:, c, :], w[:, c, :], start=(c, n) == (0, 0),
                        stop=(c, n) == (FC - 1, 2)), *((s_f, i) if (c, n) == (FC - 1, 2) else ()))

        def f_sum(i):
            wait("dve", s_f, i)
            wait("dve", s_xb, i)
            do("dve", lambda e: e.scalar_tensor_tensor(X[:, i, :], f_bank[i % 2][:, 0:D], s_f2[:, :], X[:, i, :],
                                                       ALU.mult, ALU.add), s_out, i)
            if i % STORE == STORE - 1:
                tl = slice(i + 1 - STORE, i + 1)
                wait("sp", s_out, i)
                do("sp", lambda e: e.dma_start(out_tok[:, tl, :], X[:, tl, :]), s_store, i)

        for eng in ("pe", "pool"):
            wait(eng, s_w, "ffn_weights")
        wait("pe", s_mlo, ("y", B - 1))
        turns = ((L_NORM, f_negmean), (L_NORM, f_norm), (L_HID, f_hidden), (L_ZT, f_zT), (L_OUT, f_out), (L_YT, f_yT),
                 (L_HID, f_gelu), (L_ZT, f_zhi), (L_YT, f_yhi),
                 (L_STAT, f_stats), (L_STAT, f_root), (L_ZLO, f_zlo),
                 (L_YLO, f_ylo), (0, f_y), (0, f_bias), (L_SUM, f_sum))
        for t in range(NT + L_SUM):
            for lag, fn in turns:
                if 0 <= t - lag < NT:
                    fn(t - lag)
        wait("sp", s_store, NT - 1)

        block = ctx.enter_context(nc.Block())

        @block.sync
        def _(e):
            q.replay("sp", e)

        @block.scalar
        def _(e):
            q.replay("act", e)

        @block.gpsimd
        def _(e):
            q.replay("pool", e)

        @block.vector
        def _(e):
            q.replay("dve", e)

        @block.tensor
        def _(e):
            q.replay("pe", e)


_INS = ["L0_attn_query", "L0_attn_Wq", "L0_attn_Wk", "L0_attn_Wv", "L0_attn_Wp", "L0_attn_bp",
        "L0_ffn_ln1_g", "L0_ffn_ln1_b", "L0_ffn_w1", "L0_ffn_b1", "L0_ffn_ln2_g", "L0_ffn_ln2_b", "L0_ffn_w2", "L0_ffn_b2"]


def kernel(**inputs):
    from concourse import bacc
    from concourse.bass_utils import run_bass_kernel_spmd

    nc = bacc.Bacc("TRN2", target_bir_lowering=False, num_devices=1)
    arrays, args = {}, []
    for name in _INS:
        a = np.ascontiguousarray(inputs[name])
        arrays[f"in_{name}"] = a
        args.append(nc.dram_tensor(f"in_{name}", a.shape, mybir.dt.from_np(a.dtype), kind="ExternalInput").ap())
    result = nc.dram_tensor("result", (B, N, D), F32, kind="ExternalOutput").ap()
    layer(nc, *args, result)
    r = run_bass_kernel_spmd(nc, [arrays], core_ids=[0])
    return r.results[0]["result"]
```

```python
from contextlib import ExitStack

import concourse.bass as bass
import numpy as np
from concourse import mybir

F32, F16 = mybir.dt.float32, mybir.dt.float16
ALU, ACT, AX = mybir.AluOpType, mybir.ActivationFunctionType, mybir.AxisListType
ROP = bass.bass_isa.ReduceOp

B, N, D = 32, 256, 128
H, E = 16, 64
F = 512
P = 128
NB = N // P
NT = B * NB
HC = H * E // P
FC = F // P
NH = B * H
EPS = 1e-5
TINY = 1e-20
VW = 130
GH = 4
HH = 8

Q_LEAD, MAX_LEAD, PV_LAG = 22, 19, 3
FFN_LEAD = 2
TAIL = 9
P_RING = 4
VALUE_STEPS = (3, 7, 11, 15)
FIRST_VALUE_STEPS = (-3, -2, 2, 6)
PIECE_STEPS = (0, 4, 8, 12)
XT_RING = 3


class Signal:

    def __init__(self, sem, step=1):
        self.sem, self.step, self.count, self.at = sem, step, 0, {}


class Queues:

    def __init__(self):
        self.of = {name: [] for name in ("sp", "act", "pool", "dve", "pe")}
        self.waited = {}

    def do(self, engine, fn, signal=None, key=None):
        if signal is None:
            self.of[engine].append(fn)
            return
        signal.count += signal.step
        signal.at[key] = signal.count
        self.of[engine].append(lambda e: fn(e).then_inc(signal.sem, signal.step))

    def wait(self, engine, signal, key):
        value = signal.at[key]
        if self.waited.get((engine, signal.sem), 0) >= value:
            return
        self.waited[engine, signal.sem] = value
        self.of[engine].append(lambda e: e.wait_ge(signal.sem, value))

    def replay(self, engine, e):
        for fn in self.of[engine]:
            fn(e)


def layer(nc, x_in, wq_in, wk_in, wv_in, wp_in, bp_in, g1_in, lb1_in, w1_in, b1_in,
          g2_in, lb2_in, w2_in, b2_in, out):
    ctx = ExitStack()
    with ctx:
        def sb(name, shape, dt=F32):
            return ctx.enter_context(nc.sbuf_tensor(name, shape, dt))

        def signal(name, step=1):
            return Signal(ctx.enter_context(nc.semaphore(name)), step)

        q = Queues()
        do, wait = q.do, q.wait
        bank = [ctx.enter_context(nc.psum_tensor(f"bank{i}", [P, 512], F32)) for i in range(8)]

        X = sb("X", [P, NT, D])
        ident = sb("ident", [P, P])
        Mh, Ml = sb("Mh", [P, H, D], F16), sb("Ml", [P, H, D], F16)
        Wvh, Wvl = sb("Wvh", [P, H * E], F16), sb("Wvl", [P, H * E], F16)
        Wph, Wpl = sb("Wph", [P, HC, D], F16), sb("Wpl", [P, HC, D], F16)
        T1h, T1l = sb("T1h", [P, F], F16), sb("T1l", [P, F], F16)
        T2h, T2l = sb("T2h", [P, FC, D], F16), sb("T2l", [P, FC, D], F16)
        bias2 = sb("bias2", [P, D])
        bp_all = sb("bp_all", [P, D])
        largest = sb("largest", [P, 20])
        s_exp = sb("s_exp", [P, H])
        s_y, s_f1, s_f2 = sb("s_y", [P, 1]), sb("s_f1", [P, 1]), sb("s_f2", [P, 1])
        half = sb("half", [P, 2])
        xn = sb("xn", [P, NB, D])
        xTh = [sb(f"xTh{i}", [P, N], F16) for i in range(XT_RING)]
        xTl = [sb(f"xTl{i}", [P, N], F16) for i in range(XT_RING)]
        Qh = [sb(f"Qh{i}", [P, H, N], F16) for i in range(2)]
        Ql = [sb(f"Ql{i}", [P, H, N], F16) for i in range(2)]
        negmax = [sb(f"negmax{i}", [P, P]) for i in range(2)]
        shift = [sb(f"shift{i}", [H * NB, P], F16) for i in range(2)]
        V = [sb(f"V{i}", [P, NB, H, VW], F16) for i in range(2)]
        p32 = [sb(f"p32_{i}", [P, NB, N]) for i in range(P_RING)]
        ph = [sb(f"ph{i}", [P, NB, N], F16) for i in range(P_RING)]
        pl = [sb(f"pl{i}", [P, NB, N], F16) for i in range(P_RING)]
        o_part = [sb(f"o_part{i}", [P, NB, E]) for i in range(2)]
        O = [sb(f"O{i}", [P, NB, H, E]) for i in range(2)]
        rsum = [sb(f"rsum{i}", [P, NB, H]) for i in range(2)]
        O16 = [sb(f"O16_{i}", [P, NB, 2, HH * E], F16) for i in range(H // HH)]
        OT = [sb(f"OT{i}", [P, NB, 2, HH * E // P, P], F16) for i in range(H // HH)]
        st0, mv0 = sb("st0", [P, NB, 6]), sb("mv0", [P, NB, 2])
        ve0, r0 = sb("ve0", [P, NB]), sb("r0", [P, NB])
        st1, mv1 = sb("st1", [P, NB, 6]), sb("mv1", [P, NT, 2])
        ve1, r1 = sb("ve1", [P, NT]), sb("r1", [P, NT])

        setup = ExitStack()

        def tmp(name, shape, dt=F32):
            return setup.enter_context(nc.sbuf_tensor(name, shape, dt))

        W = tmp("W", [P, 3, H * E])
        Wv_last = tmp("Wv_last", [P, H * E])
        WT = O[1][:, :, :, :].rearrange("p t h e -> p (t h e)").rearrange("p (i c d) -> p i c d", i=2, c=HC)
        M32 = O[0][:, :, :, :].rearrange("p t h e -> p (t h e)").rearrange("p (h d) -> p h d", h=H)
        Wp = tmp("Wp", [P, HC, D])
        w1, w2 = tmp("w1", [P, FC, D]), tmp("w2", [P, F])
        g1, lb1, g2, lb2 = tmp("g1", [P, 1]), tmp("lb1", [P, 1]), tmp("g2", [P, FC]), tmp("lb2", [P, FC])
        b1_all, b2_all = tmp("b1_all", [P, F]), tmp("b2_all", [P, D])
        ones = tmp("ones", [P, P])
        part = tmp("part", [P, 20])
        psums, sums = tmp("psums", [P, 2]), tmp("sums", [P, 2])
        inv = tmp("inv", [P, 20])
        clip, sc, rsc = tmp("clip", [P, 2]), tmp("sc", [P, 2]), tmp("rsc", [P, 2])
        gs2 = tmp("gs2", [P, FC])
        above, below = [tmp(f"above{i}", [P, F]) for i in range(2)], [tmp(f"below{i}", [P, F]) for i in range(2)]
        tern = [tmp(f"tern{i}", [P, F]) for i in range(2)]
        lbrep1, lbrep2 = tmp("lbrep1", [P, P]), tmp("lbrep2", [P, FC, P])
        last = tmp("last", [P, P])

        qk_loaded, v_loaded, wp_loaded, ffn_loaded, rows_loaded, bp_loaded = (
            signal(f"s_load_{n}", 16) for n in ("qk", "v", "wp", "ffn", "rows", "bp"))
        edges = [0, 2] + list(range(4, B + 1, 4))
        x_loaded = [signal(f"s_load_x{i}", 16) for i in range(len(edges) - 1)]
        x_of = {b: x_loaded[c] for c in range(len(edges) - 1) for b in range(edges[c], edges[c + 1])}
        x_tok = x_in.rearrange("b (t p) d -> p (b t) d", p=P)

        def load(dst, src, sig, key, **kw):
            do("sp", lambda e: e.dma_start(dst, src, **kw), sig, key)

        def load_w(i, src, sig):
            load(W[:, i, :].rearrange("p (h e) -> p h e", h=H), src.rearrange("h d e -> d h e"), sig, "w")

        def load_x(c):
            tl = slice(NB * edges[c], NB * edges[c + 1])
            load(X[:, tl, :], x_tok[:, tl, :], x_loaded[c], "x")

        load_w(0, wq_in, qk_loaded)
        load_w(1, wk_in, qk_loaded)
        load_x(0)
        load_w(2, wv_in, v_loaded)
        load(Wv_last[:, :].rearrange("p (h e) -> p h e", h=H), wv_in[:, D - 1, :].partition_broadcast(P), v_loaded, "w")
        load(bp_all[:, :], bp_in.partition_broadcast(P), bp_loaded, "bp")
        load_x(1)
        wp_v = wp_in.rearrange("(e c hh) o -> hh e c o", c=HC, hh=2)
        for hh in range(2):
            load(Wp[hh * E:(hh + 1) * E, :, :], wp_v[hh], wp_loaded, "wp")
        load(w1[:, :, :], w1_in.rearrange("(c p) d -> p c d", p=P), ffn_loaded, "ffn")
        load(w2[:, :], w2_in, ffn_loaded, "ffn")
        load(g1[:, :], g1_in.rearrange("(p o) -> p o", o=1), ffn_loaded, "ffn")
        load(lb1[:, :], lb1_in.rearrange("(p o) -> p o", o=1), ffn_loaded, "ffn")
        load(g2[:, :], g2_in.rearrange("(c p) -> p c", p=P), ffn_loaded, "ffn", allow_slow_non_contiguous=True)
        load(lb2[:, :], lb2_in.rearrange("(c p) -> p c", p=P), ffn_loaded, "ffn", allow_slow_non_contiguous=True)
        load(b1_all[:, :], b1_in.partition_broadcast(P), rows_loaded, "rows")
        load(b2_all[:, :], b2_in.partition_broadcast(P), rows_loaded, "rows")
        for c in range(2, len(edges) - 1):
            load_x(c)

        s_const, s_id = signal("s_const"), signal("s_ident")
        do("pool", lambda e: e.memset(ident[:, :], 0.0), s_id, "zero")
        do("pool", lambda e: e.memset(half[:, :], -0.5), s_const, "half")
        wait("pool", s_id, "zero")
        do("pool", lambda e: e.affine_select(out=ident[:, :], in_=ident[:, :], compare_op=ALU.not_equal, fill=1.0,
                                             base=0, pattern=[[-1, P]], channel_multiplier=1), s_id, "ident")
        s_dc = signal("s_dve_const")
        for i in range(2):
            do("dve", lambda e, i=i: e.memset(negmax[i][:, :], 0.0))
            do("dve", lambda e, i=i: e.memset(V[i][:, :, :, 2 * E:2 * E + 1], 1.0))
        do("dve", lambda e: e.memset(xn[:, :, D - 1:D], 1.0))
        do("dve", lambda e: e.memset(ones[:, :], 1.0), s_dc, "consts")

        s_w = signal("s_weights")
        s_hi = signal("s_weight_hi")
        s_wt, s_m, s_mc = signal("s_wt"), signal("s_m"), signal("s_m_copied")
        s_all = signal("s_all_reduced")
        n_step = [0]

        def step(fn, key=None):
            settled("dve")
            n_step[0] += 1
            do("dve", fn, s_w, n_step[0])
            if key:
                s_w.at[key] = s_w.count

        def settled(engine):
            if n_step[0]:
                wait(engine, s_w, n_step[0])

        def largest_of(dst, src, key):
            do("dve", lambda e: e.tensor_reduce(dst, src, AX.X, ALU.max, apply_absolute_value=True), s_w, key)

        def over_partitions(cols, key):
            wait("pool", s_w, key)
            do("pool", lambda e: e.partition_all_reduce(largest[:, cols], part[:, cols], P, ROP.max), s_all, key)

        def inverses(cols, key):
            wait("dve", s_all, key)
            step(lambda e: e.tensor_scalar(largest[:, cols], largest[:, cols], TINY, None, ALU.max))
            step(lambda e: e.reciprocal(inv[:, cols], largest[:, cols]))

        def high(src32, hi, key, scale=1.0):
            settled("act")
            if isinstance(scale, float):
                do("act", lambda e: e.activation(hi, src32, ACT.Copy), s_hi, key)
            else:
                do("act", lambda e: e.activation(hi, src32, ACT.Identity, scale=scale), s_hi, key)

        def low(src32, hi, lo, key, scale=None):
            wait("dve", s_hi, key)
            settled("dve")
            if scale is None:
                do("dve", lambda e: e.tensor_tensor(lo, src32, hi, ALU.subtract), s_w, key)
            else:
                do("dve", lambda e: e.scalar_tensor_tensor(lo, src32, scale, hi, ALU.mult, ALU.subtract), s_w, key)

        t_banks, m_banks = {(0, 0): bank[0], (0, 1): bank[1], (1, 0): bank[2], (1, 1): bank[4]}, bank[5:7] + bank[0:2]
        wait("pe", s_id, "ident")
        wait("pe", qk_loaded, "w")
        for j in range(2):
            for i in range(2):
                ps = t_banks[j, i]
                for c in range(4):
                    do("pe", lambda e, ps=ps, c=c, i=i, j=j: e.transpose(
                        ps[:, c * P:(c + 1) * P], W[:, i, (4 * j + c) * P:(4 * j + c + 1) * P], ident[:, :]),
                        *((s_wt, (j, i)) if c == 3 else ()))
                wait("dve", s_wt, (j, i))
                for c in range(4):
                    do("dve", lambda e, ps=ps, c=c, i=i, j=j: e.tensor_scalar(
                        WT[:, i, 4 * j + c, :], ps[:, c * P:(c + 1) * P], ps[:, c * P + D - 1:c * P + D], None,
                        ALU.subtract), *((s_w, ("WT", j, i)) if c == 3 else ()))
        M_by_pair = M32.rearrange("p (c hh) d -> p c hh d", hh=2)
        for j in range(2):
            wait("pe", s_w, ("WT", j, 1))
            for odd in range(2):
                ps, rows = m_banks[2 * j + odd], slice(odd * E, (odd + 1) * E)
                for c in range(4):
                    do("pe", lambda e, ps=ps, c=c, j=j, rows=rows: e.matmul(
                        ps[:, c * D:(c + 1) * D], WT[rows, 0, 4 * j + c, :], WT[rows, 1, 4 * j + c, :], start=True, stop=True),
                        *((s_m, (j, odd)) if c == 3 else ()))
                wait("act", s_m, (j, odd))
                do("act", lambda e, ps=ps, j=j, odd=odd: e.activation(
                    M_by_pair[:, 4 * j:4 * j + 4, odd, :], ps[:, :].rearrange("p (c d) -> p c d", c=4), ACT.Copy),
                    s_mc, (j, odd))

        heads_of = lambda j: slice(8 * j, 8 * j + 8)

        def m_largest(j):
            wait("dve", s_mc, (j, 1))
            largest_of(part[:, heads_of(j)], M32[:, heads_of(j), :], ("part", j))
            over_partitions(heads_of(j), ("part", j))

        def m_scaled(j):
            hs = heads_of(j)
            inverses(hs, ("part", j))
            do("dve", lambda e: e.tensor_scalar(s_exp[:, hs], largest[:, hs], float(E) ** -0.5, None, ALU.mult))
            step(lambda e: e.tensor_tensor(M32[:, hs, :], M32[:, hs, :],
                                           inv[:, hs].unsqueeze(2).to_broadcast([P, 8, D]), ALU.mult))
            high(M32[:, hs, :], Mh[:, hs, :], ("M", j))

        def m_low(j):
            low(M32[:, heads_of(j), :], Mh[:, heads_of(j), :], Ml[:, heads_of(j), :], ("M", j))

        def v_less_last():
            wait("pool", v_loaded, "w")
            do("pool", lambda e: e.tensor_tensor(W[:, 2, :], W[:, 2, :], Wv_last[:, :], ALU.subtract), s_all, "Wv_less")

        def v_largest():
            wait("dve", s_all, "Wv_less")
            largest_of(part[:, 16:17], W[:, 2, :], "part_v")
            over_partitions(slice(16, 17), "part_v")

        def v_split():
            inverses(slice(16, 17), "part_v")
            settled("act")
            do("act", lambda e: e.activation(W[:, 2, :], W[:, 2, :], ACT.Identity, scale=inv[:, 16:17]), s_hi, "Wv_scaled")
            wait("act", s_hi, "Wv_scaled")
            do("act", lambda e: e.activation(Wvh[:, :], W[:, 2, :], ACT.Copy), s_hi, "Wv")
            wait("pool", s_hi, "Wv")
            do("pool", lambda e: e.tensor_tensor(Wvl[:, :], W[:, 2, :], Wvh[:, :], ALU.subtract), s_all, "Wv")

        def p_largest():
            wait("dve", wp_loaded, "wp")
            largest_of(part[:, 17:18], Wp[:, :, :].rearrange("p c o -> p (c o)"), "part_p")
            over_partitions(slice(17, 18), "part_p")

        def p_high():
            inverses(slice(17, 18), "part_p")
            step(lambda e: e.tensor_tensor(s_y[:, :], largest[:, 16:17], largest[:, 17:18], ALU.mult))
            high(Wp[:, :, :], Wph[:, :, :], "Wp", inv[:, 17:18])

        def p_low():
            low(Wp[:, :, :], Wph[:, :, :], Wpl[:, :, :], "Wp", inv[:, 17:18])

        s_ft, s_fb = signal("s_ffn_t"), signal("s_ffn_bias")

        def sum_w1():
            wait("dve", ffn_loaded, "ffn")
            do("dve", lambda e: e.tensor_reduce(psums[:, 0:1], w1[:, :, :].rearrange("p c d -> p (c d)"), AX.X, ALU.add,
                                                apply_absolute_value=True))

        def sum_w2():
            do("dve", lambda e: e.tensor_reduce(psums[:, 1:2], w2[:, :], AX.X, ALU.add, apply_absolute_value=True),
               s_w, "psums")
            wait("pool", s_w, "psums")
            do("pool", lambda e: e.partition_all_reduce(sums[:, :], psums[:, :], P, ROP.add), s_all, "sums")
            largest_of(part[:, 19:20], g2[:, :], "part_g")
            over_partitions(slice(19, 20), "part_g")

        def w_scales():
            inverses(slice(19, 20), "part_g")
            wait("dve", s_all, "sums")
            step(lambda e: e.tensor_scalar(clip[:, :], sums[:, :], 1.0 / (F * D), 1e-5, ALU.mult, ALU.max))
            step(lambda e: e.reciprocal(sc[:, :], clip[:, :]))

        def f_scales():
            step(lambda e: e.reciprocal(rsc[:, :], sc[:, :]))
            step(lambda e: e.tensor_scalar(gs2[:, :], g2[:, :], inv[:, 19:20], None, ALU.mult))
            step(lambda e: e.tensor_tensor(s_f2[:, :], rsc[:, 1:2], largest[:, 19:20], ALU.mult))

        def ternary(i):
            m = misc_take()
            wait("pe", ffn_loaded, "ffn")
            for c in range(FC):
                src = w1[:, c, :] if i == 0 else w2[:, c * P:(c + 1) * P]
                do("pe", lambda e, c=c, src=src: e.transpose(m[:, c * P:(c + 1) * P], src, ident[:, :]),
                   *((s_ft, i) if c == FC - 1 else ()))
            misc_read(s_w, ("ternary", i))

            def compare():
                wait("dve", s_ft, i)
                settled("dve")
                do("dve", lambda e: e.tensor_scalar(above[i][:, :], m[:, :], sc[:, i:i + 1], 0.5, ALU.mult, ALU.is_gt))
                step(lambda e: e.tensor_scalar(below[i][:, :], m[:, :], sc[:, i:i + 1], -0.5, ALU.mult, ALU.is_lt),
                     ("ternary", i))
            later.append(compare)

        def ternary_out(i):
            step(lambda e: e.tensor_tensor(tern[i][:, :], above[i][:, :], below[i][:, :], ALU.subtract))

        T1 = above[0]

        def gains1():
            step(lambda e: e.tensor_scalar(T1[:, :], tern[0][:, :], g1[:, :], None, ALU.mult))
            step(lambda e: e.tensor_copy(last[:, :], ident[:, D - 1:D].to_broadcast([P, P])))

        def shared_product(stationary, moving, key, fn):
            m = misc_take()
            settled("pe")
            do("pe", lambda e: e.matmul(m[:, :], stationary[:, :], moving[:, :], start=True, stop=True), s_fb, key)
            misc_read(s_w, key)

            def out():
                wait("dve", s_fb, key)
                step(lambda e: fn(e, m), key)
            later.append(out)

        def less_last_row():
            shared_product(last, T1, "T1_last", lambda e, m: e.tensor_tensor(T1[:, :], T1[:, :], m[:, :], ALU.subtract))

        def bias1_product():
            step(lambda e: e.tensor_scalar(lbrep1[:, :], ones[:, :], lb1[:, :], None, ALU.mult))
            wait("dve", rows_loaded, "rows")
            shared_product(lbrep1, tern[0], "bias1", lambda e, m: e.scalar_tensor_tensor(
                b1_all[:, :], b1_all[:, :], sc[:, 0:1], m[:, :], ALU.mult, ALU.add))

        def bias1_row():
            step(lambda e: e.scalar_tensor_tensor(T1[:, :], b1_all[:, :], ident[:, D - 1:D], T1[:, :], ALU.mult, ALU.add))

        def t1_largest():
            settled("dve")
            largest_of(part[:, 18:19], T1[:, :], "part_t1")
            over_partitions(slice(18, 19), "part_t1")

        def t1_split():
            inverses(slice(18, 19), "part_t1")
            step(lambda e: e.tensor_tensor(s_f1[:, :], rsc[:, 0:1], largest[:, 18:19], ALU.mult))
            high(T1[:, :], T1h[:, :], "T1", inv[:, 18:19])
            later.append(lambda: low(T1[:, :], T1h[:, :], T1l[:, :], "T1", inv[:, 18:19]))

        def gains2():
            settled("dve")
            for c in range(FC):
                fn = (lambda e, c=c: e.tensor_scalar(above[1][:, c * D:(c + 1) * D], tern[1][:, c * D:(c + 1) * D],
                                                     gs2[:, c:c + 1], None, ALU.mult))
                step(fn) if c == FC - 1 else do("dve", fn)
            hi, lo = (T[:, :, :].rearrange("p c d -> p (c d)") for T in (T2h, T2l))
            high(above[1][:, :], hi, "T2")
            later.append(lambda: low(above[1][:, :], hi, lo, "T2"))

        def bias2_product():
            settled("dve")
            for c in range(FC):
                fn = lambda e, c=c: e.tensor_scalar(lbrep2[:, c, :], ones[:, :], lb2[:, c:c + 1], None, ALU.mult)
                step(fn) if c == FC - 1 else do("dve", fn)
            m = misc_take()
            settled("pe")
            for c in range(FC):
                do("pe", lambda e, c=c: e.matmul(m[:, 0:D], lbrep2[:, c, :], tern[1][:, c * D:(c + 1) * D],
                                                 start=c == 0, stop=c == FC - 1), *((s_fb, 1) if c == FC - 1 else ()))
            misc_read(s_w, "ffn_weights")

            def add():
                wait("dve", s_fb, 1)
                do("dve", lambda e: e.scalar_tensor_tensor(bias2[:, :], m[:, 0:D], rsc[:, 1:2], b2_all[:, :],
                                                           ALU.mult, ALU.add), s_w, "ffn_weights")
            later.append(add)

        pieces = [sum_w1, sum_w2, w_scales, f_scales, lambda: ternary(0), lambda: ternary_out(0), lambda: ternary(1),
                  lambda: ternary_out(1), gains1, less_last_row, bias1_product, bias1_row, t1_largest, t1_split,
                  gains2, bias2_product]
        work_at = {(b, s): [] for b in range(-2, B + 1) for s in range(H)}
        for n, fn in enumerate(pieces):
            work_at[1 + n // len(PIECE_STEPS), PIECE_STEPS[n % len(PIECE_STEPS)]].append(fn)
        for t, fn in ((-22, lambda: m_scaled(1)), (-20, lambda: m_low(1)), (-15, v_largest), (-12, v_split),
                      (8, p_largest), (12, p_high), (18, p_low)):
            work_at[divmod(t, H)].append(fn)

        s_st, s_r0, s_xn, s_xbp = signal("s_ln_stats"), signal("s_ln_root"), signal("s_xn"), signal("s_x_plus_bp")
        s_misc = signal("s_misc_ready")
        s_mhi, s_mlo = signal("s_misc_hi"), signal("s_misc_lo")
        s_q, s_qhi, s_qlo = signal("s_q"), signal("s_q_hi"), signal("s_q_lo")
        s_q32, s_qlp = signal("s_q_copied"), signal("s_q_lo_pool")
        s_ms, s_mx = signal("s_max_scores"), signal("s_max")
        s_sh = [signal(f"s_shift{i}", 16) for i in range(2)]
        s_sc, s_exp_done, s_ph, s_pl = signal("s_scores"), signal("s_exp"), signal("s_p_hi"), signal("s_p_lo")
        s_pv, s_o1, s_o, s_on = signal("s_pv"), signal("s_o_part"), signal("s_o"), signal("s_o_normal")
        s_x1 = signal("s_x1_stats")
        s_ot = [signal(f"s_outputs_transposed{c}", 16) for c in range(H // HH)]
        sc_bank, pv_bank, misc_banks = bank[0:2], bank[4:6], (bank[3], bank[7])
        ms_bank = lambda g: bank[5] if g < MAX_LEAD and g % 2 else bank[2]
        q_bank = lambda g: bank[4] if g < Q_LEAD and g // 2 % 2 else bank[6]
        early = lambda g: g < Q_LEAD
        q_low_of = lambda g: s_qlp if early(g) else s_qlo
        q_read_of = lambda g: s_q32 if early(g) else s_qlo
        q_copy = lambda g: p32[g // 2 % P_RING]
        ms_last, q_last = {}, {}
        misc_reader, misc_turn = [None, None], [0]

        def misc_take():
            misc_turn[0] ^= 1
            if misc_reader[misc_turn[0]]:
                wait("pe", *misc_reader[misc_turn[0]])
            return misc_banks[misc_turn[0]]

        def misc_read(sig, key):
            misc_reader[misc_turn[0]] = (sig, key)

        later = []

        def norm_stats(b):
            wait("dve", x_of[b], "x")
            if b:
                wait("dve", s_r0, b - 1)
            for t in range(NB):
                do("dve", lambda e, t=t: e.bn_stats(st0[:, t, :], X[:, NB * b + t, :]), s_st, ("st", b))
            wait("dve", s_st, ("st", b))
            for t in range(NB):
                do("dve", lambda e, t=t: e.bn_aggr(mv0[:, t, :], st0[:, t, :]), s_st, ("mv", b))

        def norm_root(b):
            wait("pool", s_st, ("mv", b))
            wait("pool", s_const, "half")
            do("pool", lambda e: e.tensor_scalar(ve0[:, :], mv0[:, :, 1], EPS, None, ALU.add), s_r0, ("ve", b))
            wait("pool", s_r0, ("ve", b))
            if b:
                wait("pool", s_xn, b - 1)
            do("pool", lambda e: e.tensor_tensor(r0[:, :], ve0[:, :], half[:, :], ALU.pow), s_r0, b)

        def norm_apply(b):
            wait("dve", s_r0, b)
            wait("dve", s_st, ("mv", b))
            if b:
                wait("dve", s_misc, ("xT", b - 1))
            for t in range(NB):
                do("dve", lambda e, t=t: e.tensor_scalar(xn[:, t, 0:D - 1], X[:, NB * b + t, 0:D - 1], mv0[:, t, 0:1],
                                                         r0[:, t:t + 1], ALU.subtract, ALU.mult), s_xn, b)

        def add_bp(b):
            wait("pool", s_xn, b)
            wait("pool", bp_loaded, "bp")
            tiles = X[:, NB * b:NB * b + NB, :]
            do("pool", lambda e: e.tensor_tensor(tiles, tiles, bp_all[:, :].unsqueeze(1).to_broadcast([P, NB, D]), ALU.add),
               s_xbp, b)

        def low_part(lo, src, hi, key):
            def fn():
                wait("dve", s_mhi, key)
                do("dve", lambda e: e.tensor_tensor(lo, src, hi, ALU.subtract), s_mlo, key)
            misc_read(s_mlo, key)
            later.append(fn)

        def x_transposed(b):
            r = b % XT_RING
            misc = misc_take()
            wait("pe", s_xn, b)
            wait("pe", s_dc, "consts")
            for t in range(NB):
                do("pe", lambda e, t=t: e.transpose(misc[:, t * P:(t + 1) * P], xn[:, t, :], ident[:, :]),
                   *((s_misc, ("xT", b)) if t == NB - 1 else ()))
            wait("act", s_misc, ("xT", b))
            if b >= XT_RING:
                wait("act", s_sc, H * (b - XT_RING) + H - 1)
            do("act", lambda e: e.activation(xTh[r][:, :], misc[:, 0:N], ACT.Copy), s_mhi, ("xT", b))
            low_part(xTl[r][:, :], misc[:, 0:N], xTh[r][:, :], ("xT", b))

        def queries(g):
            b, h, r = g // H, g % H, (g // H) % XT_RING
            wait("pe", s_mlo, ("xT", b))
            wait("pe", s_w, ("M", h // 8))
            dst = q_bank(g)
            if id(dst) in q_last:
                wait("pe", q_read_of(q_last[id(dst)]), q_last[id(dst)])
            q_last[id(dst)] = g
            for j in range(2):
                o = dst[:, j * N:(j + 1) * N]
                for n, (m, xt) in enumerate(((Mh, xTh), (Mh, xTl), (Ml, xTh))):
                    do("pe", lambda e, o=o, m=m, xt=xt, j=j, n=n: e.matmul(
                        o, m[:, h + j, :], xt[r][:, :], start=n == 0, stop=n == 2),
                        *((s_q, g) if (j, n) == (1, 2) else ()))

        def queries_out(g):
            b, h = g // H, g % H
            wait("act", s_q, g)
            if b >= 2:
                wait("act", s_sc, g + 1 - 2 * H)
            src = q_bank(g)[:, :].rearrange("p (j n) -> p j n", j=2)
            hi, lo = Qh[b % 2][:, h:h + 2, :], Ql[b % 2][:, h:h + 2, :]
            do("act", lambda e: e.activation(hi, src, ACT.Copy), s_qhi, g)

            if early(g):
                if g >= 2 * P_RING:
                    wait("act", s_qlp, g - 2 * P_RING)
                do("act", lambda e: e.activation(q_copy(g)[:, :, :], src, ACT.Copy), s_q32, g)
                wait("pool", s_q32, g)
                do("pool", lambda e: e.tensor_tensor(lo, q_copy(g)[:, :, :], hi, ALU.subtract), s_qlp, g)
                return

            def q_low():
                wait("dve", s_qhi, g)
                do("dve", lambda e: e.tensor_tensor(lo, src, hi, ALU.subtract), s_qlo, g)
            later.append(q_low)

        def max_scores(g):
            b, h = g // H, g % H
            wait("pe", s_qhi, g - g % 2)
            dst = ms_bank(g)
            if id(dst) in ms_last:
                wait("pe", s_mx, ms_last[id(dst)])
            ms_last[id(dst)] = g
            for t in range(NB):
                do("pe", lambda e, t=t: e.matmul(dst[:, t * N:(t + 1) * N], Qh[b % 2][:, h, t * P:(t + 1) * P],
                                                 xTh[b % XT_RING][:, :], start=True, stop=True),
                   *((s_ms, g) if t == NB - 1 else ()))

        def max_out(g):
            b, h = g // H, g % H
            wait("dve", s_ms, g)
            if b >= 2:
                wait("dve", s_misc, ("shift", b - 2))
            do("dve", lambda e: e.tensor_reduce(negmax[b % 2][:, NB * h:NB * h + NB],
                                                ms_bank(g)[:, :].rearrange("p (t m) -> p t m", t=NB),
                                                AX.X, ALU.max, negate=True), s_mx, g)

        def shift_rows(b):
            misc = misc_take()
            wait("pe", s_mx, H * b + H - 1)
            do("pe", lambda e: e.transpose(misc[:, 0:P], negmax[b % 2][:, :], ident[:, :]), s_misc, ("shift", b))
            misc_read(s_mlo, ("shift", b))

            def out_and_over():
                wait("dve", s_misc, ("shift", b))
                if b >= 2:
                    wait("dve", s_sh[b % 2], b - 2)
                do("dve", lambda e: e.tensor_copy(shift[b % 2][:, :], misc[0:H * NB, 0:P]), s_mlo, ("shift", b))
                wait("sp", s_mlo, ("shift", b))
                wait("sp", q_low_of(H * b + H - 2), H * b + H - 2)
                do("sp", lambda e: e.dma_start(Qh[b % 2][D - 1:D, :, :].rearrange("p h (t n) -> p (h t) n", t=NB),
                                               shift[b % 2][:, :]), s_sh[b % 2], b)
            later.append(out_and_over)

        def scores(g):
            b, h, r = g // H, g % H, (g // H) % XT_RING
            wait("pe", s_sh[b % 2], b)
            wait("pe", q_low_of(g - g % 2), g - g % 2)
            if g >= 2:
                wait("pe", s_exp_done, g - 2)
            for t in range(NB):
                o = sc_bank[g % 2][:, t * N:(t + 1) * N]
                for n, (xt, qq) in enumerate(((xTh, Qh), (xTh, Ql), (xTl, Qh))):
                    do("pe", lambda e, o=o, xt=xt, qq=qq, t=t, n=n: e.matmul(
                        o, xt[r][:, t * P:(t + 1) * P], qq[b % 2][:, h, :], start=n == 0, stop=n == 2),
                        *((s_sc, g) if (t, n) == (NB - 1, 2) else ()))

        def exps(g):
            i = g % P_RING
            wait("act", s_sc, g)
            if g == 0:
                wait("act", s_qlp, Q_LEAD - 2)
            if g >= P_RING:
                wait("act", s_pl, g - P_RING)
                wait("act", s_ph, g - P_RING)
            do("act", lambda e: e.activation(p32[i][:, :, :], sc_bank[g % 2][:, :].rearrange("p (t n) -> p t n", t=NB),
                                             ACT.Exp, scale=s_exp[:, g % H:g % H + 1]), s_exp_done, g)

        def split_p(g):
            i = g % P_RING
            wait("act", s_exp_done, g)
            if g >= P_RING:
                wait("act", s_pv, g - P_RING)
                wait("pool", s_pv, g - P_RING)
            do("act", lambda e: e.activation(ph[i][:, :, :], p32[i][:, :, :], ACT.Copy), s_ph, g)
            wait("pool", s_ph, g)
            do("pool", lambda e: e.tensor_tensor(pl[i][:, :, :], p32[i][:, :, :], ph[i][:, :, :], ALU.subtract), s_pl, g)

        def values(b, m, half_):
            r, cols = b % XT_RING, slice(half_ * 512, half_ * 512 + 512)
            h0 = half_ * 8
            misc = misc_take()
            wait("pe", s_mlo, ("xT", b))
            wait("pe", s_all, "Wv")
            for n, (xt, w) in enumerate(((xTh, Wvh), (xTh, Wvl), (xTl, Wvh))):
                do("pe", lambda e, xt=xt, w=w, n=n: e.matmul(misc[:, :], xt[r][:, m * P:(m + 1) * P], w[:, cols],
                                                             start=n == 0, stop=n == 2),
                   *((s_misc, ("V", b, m, half_)) if n == 2 else ()))
            key = ("V", b, m, half_)
            src = misc[:, :].rearrange("p (h e) -> p h e", h=8)
            hi, lo = V[b % 2][:, m, h0:h0 + 8, E:2 * E], V[b % 2][:, m, h0:h0 + 8, 0:E]
            wait("act", s_misc, key)
            if b >= 2:
                wait("act", s_pv, H * (b - 2) + H - 1)
            do("act", lambda e: e.activation(hi, src, ACT.Copy), s_mhi, key)
            low_part(lo, src, hi, key)

        def weighted(g):
            b, h, i = g // H, g % H, g % P_RING
            wait("pe", s_pl, g)
            for m in range(NB):
                wait("pe", s_mlo, ("V", b, m, h // 8))
            if g >= 2:
                wait("pe", s_o, g - 2)
            elif id(pv_bank[g]) in q_last:
                wait("pe", s_q32, q_last[id(pv_bank[g])])
            elif id(pv_bank[g]) in ms_last:
                wait("pe", s_mx, ms_last[id(pv_bank[g])])
            for t in range(NB):
                for m in range(NB):
                    for pp, lo in ((ph, 0), (pl, E)):
                        do("pe", lambda e, t=t, m=m, pp=pp, lo=lo: e.matmul(
                            pv_bank[g % 2][:, t * N + lo:t * N + 2 * E + 1], pp[i][:, m, t * P:(t + 1) * P],
                            V[b % 2][:, m, h, lo:2 * E + 1], start=m == 0 and lo == 0, stop=m == NB - 1 and lo == E),
                            *((s_pv, g) if (t, m, lo) == (NB - 1, NB - 1, E) else ()))

        def weighted_out(g):
            b, h = g // H, g % H
            src = pv_bank[g % 2][:, :].rearrange("p (t n) -> p t n", t=NB)
            wait("act", s_pv, g)
            if g >= 2:
                wait("act", s_o, g - 2)
            do("act", lambda e: e.activation(o_part[g % 2][:, :, :], src[:, :, E:2 * E], ACT.Copy), s_o1, g)

            def add():
                wait("dve", s_o1, g)
                if b >= 2:
                    wait("dve", s_mhi, ("O", b - 2, h // GH))
                do("dve", lambda e: e.reciprocal(rsum[b % 2][:, :, h], src[:, :, 2 * E]))
                do("dve", lambda e: e.tensor_tensor(O[b % 2][:, :, h, :], src[:, :, 0:E], o_part[g % 2][:, :, :], ALU.add),
                   s_o, g)
            later.append(add)

        def normalise(b, k):
            h0 = GH * k
            wait("pool", s_o, H * b + h0 + GH - 1)
            tile = O[b % 2][:, :, h0:h0 + GH, :]
            do("pool", lambda e: e.tensor_tensor(tile, tile, rsum[b % 2][:, :, h0:h0 + GH].unsqueeze(3)
                                                 .to_broadcast([P, NB, GH, E]), ALU.mult), s_on, (b, k))

        def split_outputs(b, k):
            c, j = divmod(k, HH // GH)
            cols = slice(j * GH * E, (j + 1) * GH * E)
            src = O[b % 2][:, :, GH * k:GH * k + GH, :].rearrange("p t h e -> p t (h e)")
            hi, lo = O16[c][:, :, 0, cols], O16[c][:, :, 1, cols]
            wait("act", s_on, (b, k))
            if b:
                wait("act", s_ot[c], b - 1)
            do("act", lambda e: e.activation(hi, src, ACT.Copy), s_mhi, ("O", b, k))

            def o_low():
                wait("dve", s_mhi, ("O", b, k))
                do("dve", lambda e: e.tensor_tensor(lo, src, hi, ALU.subtract), s_mlo, ("O", b, k))
            later.append(o_low)

        def transpose_outputs(b, c):
            wait("sp", s_mlo, ("O", b, (c + 1) * HH // GH - 1))
            if b:
                wait("sp", s_misc, ("y", b - 1))
            do("sp", lambda e: e.dma_start_transpose(OT[c][:, :, :, :, :].rearrange("p t s c n -> p (t s c) n"),
                                                     O16[c][:, :, :, :].rearrange("p t s f -> p (t s f)")), s_ot[c], b)

        y_bank = [None]

        def project(b, t):
            if t == 0:
                y_bank[0] = misc_take()
                for c in range(H // HH):
                    wait("pe", s_ot[c], b)
                wait("pe", s_w, "Wp")
            misc = y_bank[0]
            for c in range(HC):
                for n, (part_, w) in enumerate(((0, Wph), (0, Wpl), (1, Wph))):
                    o = OT[c // (HC * HH // H)][:, t, part_, c % (HC * HH // H), :]
                    do("pe", lambda e, c=c, n=n, o=o, w=w: e.matmul(
                        misc[:, t * D:(t + 1) * D], o, w[:, c, :],
                        start=(c, n) == (0, 0), stop=(c, n) == (HC - 1, 2)),
                        *((s_misc, ("y", b)) if (t, c, n) == (NB - 1, HC - 1, 2) else ()))

        def residual(b):
            misc = y_bank[0]
            tiles = X[:, NB * b:NB * b + NB, :]

            def add():
                wait("dve", s_misc, ("y", b))
                wait("dve", s_xbp, b)
                do("dve", lambda e: e.scalar_tensor_tensor(tiles, misc[:, 0:NB * D].rearrange("p (t d) -> p t d", t=NB),
                                                           s_y[:, :], tiles, ALU.mult, ALU.add), s_mlo, ("y", b))
            later.append(add)
            misc_reader[misc_banks.index(misc)] = (s_mlo, ("y", b))

        def ffn_stats(b):
            wait("dve", s_mlo, ("y", b))
            for t in range(NB):
                do("dve", lambda e, t=t: e.bn_stats(st1[:, t, :], X[:, NB * b + t, :]), s_x1, ("st", b))
            wait("dve", s_x1, ("st", b))
            for t in range(NB):
                do("dve", lambda e, t=t: e.bn_aggr(mv1[:, NB * b + t, :], st1[:, t, :]), s_x1, ("mv", b))

        s_r1 = signal("s_ffn_root")

        def ffn_root(b):
            tl = slice(NB * b, NB * b + NB)
            wait("pool", s_x1, ("mv", b))
            do("pool", lambda e: e.tensor_scalar(ve1[:, tl], mv1[:, tl, 1], 1.0 + EPS, EPS * EPS, ALU.mult, ALU.add),
               s_r1, ("ve", b))
            wait("pool", s_r1, ("ve", b))
            do("pool", lambda e: e.tensor_tensor(r1[:, tl], ve1[:, tl], half[:, :], ALU.pow), s_r1, b)

        def batch_work(b, s):
            ok = lambda c: 0 <= c < B
            if s == 9 and 3 <= b + 3 < B or (b, s) == (0, 2):
                norm_stats(b + 3 if s == 9 else 2)
                norm_root(b + 3 if s == 9 else 2)
            if s == 10 and 3 <= b + 3 < B or (b, s) in ((0, 4), (-1, 4)):
                norm_apply(b + 3 if s == 10 else b + 2)
                add_bp(b + 3 if s == 10 else b + 2)
            if s == 6 and ok(b + 2) and b >= -1:
                x_transposed(b + 2)
            if s in VALUE_STEPS and 1 <= b + 1 < B:
                n = VALUE_STEPS.index(s)
                values(b + 1, n % 2, n // 2)
            if H * b + s in FIRST_VALUE_STEPS:
                n = FIRST_VALUE_STEPS.index(H * b + s)
                values(0, n % 2, n // 2)
            if s == 13 and ok(b + 1):
                shift_rows(b + 1)
            for k, (at, back) in enumerate(((7, 0), (11, 0), (15, 0), (3, 1))):
                if s == at and ok(b - back):
                    normalise(b - back, k)
            split_last, transpose_last, project_at, stats_at = (5, 6, 9, 11) if b < B else (4, 5, 7, 8)
            if s == project_at and ok(b - 1):
                project(b - 1, 0)
                project(b - 1, 1)
                residual(b - 1)
            for k, (at, back) in enumerate(((9, 0), (13, 0), (1, 1), (split_last, 1))):
                if s == at and ok(b - back):
                    split_outputs(b - back, k)
            for c, (at, back) in enumerate(((14, 0), (transpose_last, 1))):
                if s == at and ok(b - back):
                    transpose_outputs(b - back, c)
            for fn in work_at[b, s]:
                fn()
            if s == stats_at and ok(b - 1):
                ffn_stats(b - 1)
                ffn_root(b - 1)

        live = lambda g: 0 <= g < NH
        norm_stats(0)
        norm_root(0)
        m_largest(0)
        norm_apply(0)
        add_bp(0)
        x_transposed(0)
        m_scaled(0)
        m_largest(1)
        v_less_last()
        later.pop()()
        m_low(0)
        norm_stats(1)
        norm_root(1)

        def attention_step(t):
            held, later[:] = list(later), []
            if live(t - 1 + MAX_LEAD):
                max_out(t - 1 + MAX_LEAD)
            for fn in held:
                fn()
            if live(t):
                scores(t)
                exps(t)
            if live(t - PV_LAG):
                weighted(t - PV_LAG)
                weighted_out(t - PV_LAG)
            if live(t):
                split_p(t)
            if live(t + MAX_LEAD):
                max_scores(t + MAX_LEAD)
            if t % 2 == 0 and live(t + Q_LEAD):
                queries(t + Q_LEAD)
                queries_out(t + Q_LEAD)
            batch_work(t // H, t % H)

        for t in range(-Q_LEAD, NH - FFN_LEAD):
            attention_step(t)
        setup.close()

        L_YT, L_YLO, L_HID, L_STAT, L_NORM, L_ZT, L_ZLO, L_OUT, L_SUM = 1, 2, 3, 4, 6, 7, 8, 9, 10
        A_RING = 5
        y = [sb(f"y{i}", [P, D]) for i in range(2)]
        yTh = [sb(f"yTh{i}", [P, P], F16) for i in range(3)]
        yTl = [sb(f"yTl{i}", [P, P], F16) for i in range(3)]
        a = [sb(f"a{i}", [P, F]) for i in range(A_RING)]
        z = [sb(f"z{i}", [P, F]) for i in range(2)]
        zTh = [sb(f"zTh{i}", [P, FC, P], F16) for i in range(3)]
        zTl = [sb(f"zTl{i}", [P, FC, P], F16) for i in range(3)]
        st2 = [sb(f"st2_{i}", [P, 6]) for i in range(2)]
        mv2 = [sb(f"mv2_{i}", [P, 2]) for i in range(A_RING)]
        ve2 = [sb(f"ve2_{i}", [P, 1]) for i in range(A_RING)]
        r2 = [sb(f"r2_{i}", [P, 1]) for i in range(A_RING)]
        nm2 = [sb(f"nm2_{i}", [P, 1]) for i in range(A_RING)]
        s_y1, s_yt, s_yhi, s_ylo = signal("s_ffn_y"), signal("s_ffn_yT"), signal("s_ffn_y_hi"), signal("s_ffn_y_lo")
        s_pre, s_a, s_st2, s_r2, s_nm2 = (signal(f"s_ffn_{n}") for n in ("pre", "gelu", "stats2", "root2", "negmean"))
        s_z, s_zt, s_zhi, s_zlo = (signal(f"s_ffn_{n}") for n in ("z", "zT", "z_hi", "z_lo"))
        s_xb, s_f, s_out = signal("s_ffn_x_plus_bias"), signal("s_ffn_out"), signal("s_ffn_sum")
        s_store = signal("s_store", 16)
        yT_bank, pre_bank, z_bank = (bank[2], bank[6]), bank[0:2], bank[4:6]
        STORE = 4
        out_tok = out.rearrange("b (t p) d -> p (b t) d", p=P)

        def f_bank(i):
            y_at = misc_banks.index(y_bank[0])
            return misc_banks[y_at if i % 2 else 1 - y_at]

        def free(engine, sig, i, ring):
            if i >= ring:
                wait(engine, sig, i - ring)

        def f_y(i):
            wait("dve", s_r1, i // NB)
            free("dve", s_yt, i, 2)
            do("dve", lambda e: e.tensor_scalar(y[i % 2][:, 0:D - 1], X[:, i, 0:D - 1], mv1[:, i, 0:1], r1[:, i:i + 1],
                                                ALU.subtract, ALU.mult), s_y1, i)

        def f_bias(i):
            wait("pool", s_y1, i)
            do("pool", lambda e: e.tensor_tensor(X[:, i, :], X[:, i, :], bias2[:, :], ALU.add), s_xb, i)

        def f_yT(i):
            wait("pe", s_y1, i)
            wait("pe", s_mx, NH - 1)
            wait("pe", s_qlo, NH - 2)
            free("pe", s_ylo, i, 2)
            do("pe", lambda e: e.transpose(yT_bank[i % 2][:, 0:P], y[i % 2][:, :], ident[:, :]), s_yt, i)

        def f_yhi(i):
            wait("act", s_yt, i)
            free("act", s_pre, i, 3)
            do("act", lambda e: e.activation(yTh[i % 3][:, :], yT_bank[i % 2][:, 0:P], ACT.Copy), s_yhi, i)

        def f_ylo(i):
            wait("dve", s_yhi, i)
            free("dve", s_pre, i, 3)
            do("dve", lambda e: e.tensor_tensor(yTl[i % 3][:, :], yT_bank[i % 2][:, 0:P], yTh[i % 3][:, :], ALU.subtract),
               s_ylo, i)

        def f_hidden(i):
            wait("pe", s_ylo, i)
            wait("pe", s_exp_done, NH - 1)
            free("pe", s_a, i, 2)
            o = pre_bank[i % 2][:, :]
            do("pe", lambda e: e.matmul(o, yTh[i % 3][:, :], T1h[:, :], start=True, stop=False))
            do("pe", lambda e: e.matmul(o, yTh[i % 3][:, :], T1l[:, :], start=False, stop=False))
            do("pe", lambda e: e.matmul(o, yTl[i % 3][:, :], T1h[:, :], start=False, stop=True), s_pre, i)

        def f_gelu(i):
            wait("act", s_pre, i)
            free("act", s_z, i, A_RING)
            free("act", s_st2, i, A_RING)
            do("act", lambda e: e.activation(a[i % A_RING][:, :], pre_bank[i % 2][:, :], ACT.Gelu, scale=s_f1[:, :]), s_a, i)

        def f_stats(i):
            k = i % A_RING
            wait("dve", s_a, i)
            free("dve", s_st2, i, 2)
            do("dve", lambda e: e.bn_stats(st2[i % 2][:, :], a[k][:, :]), s_st2, ("st", i))

        def f_variance(i):
            k = i % A_RING
            wait("dve", s_st2, ("st", i))
            free("dve", s_r2, i, A_RING)
            free("dve", s_nm2, i, A_RING)
            do("dve", lambda e: e.bn_aggr(mv2[k][:, :], st2[i % 2][:, :]), s_st2, i)

        def f_root(i):
            k = i % A_RING
            wait("pool", s_st2, i)
            do("pool", lambda e: e.tensor_scalar(ve2[k][:, :], mv2[k][:, 1:2], EPS, None, ALU.add), s_r2, ("ve", i))
            wait("pool", s_r2, ("ve", i))
            free("pool", s_z, i, A_RING)
            free("pool", s_nm2, i, A_RING)
            do("pool", lambda e: e.tensor_tensor(r2[k][:, :], ve2[k][:, :], half[:, 0:1], ALU.pow), s_r2, i)

        def f_negmean(i):
            k = i % A_RING
            wait("pool", s_r2, i)
            do("pool", lambda e: e.tensor_scalar(nm2[k][:, :], mv2[k][:, 0:1], r2[k][:, :], -1.0, ALU.mult, ALU.mult),
               s_nm2, i)

        def f_norm(i):
            k = i % A_RING
            wait("act", s_nm2, i)
            free("act", s_zt, i, 2)
            do("act", lambda e: e.activation(z[i % 2][:, :], a[k][:, :], ACT.Identity, scale=r2[k][:, :], bias=nm2[k][:, :]),
               s_z, i)

        def f_zT(i):
            wait("pe", s_z, i)
            wait("pe", s_o, NH - 1)
            free("pe", s_zlo, i, 2)
            for c in range(FC):
                do("pe", lambda e, c=c: e.transpose(z_bank[i % 2][:, c * P:(c + 1) * P], z[i % 2][:, c * P:(c + 1) * P],
                                                    ident[:, :]), *((s_zt, i) if c == FC - 1 else ()))

        z_ps = lambda i: z_bank[i % 2][:, :].rearrange("p (c n) -> p c n", c=FC)

        def f_zhi(i):
            wait("act", s_zt, i)
            free("act", s_f, i, 3)
            do("act", lambda e: e.activation(zTh[i % 3][:, :, :], z_ps(i), ACT.Copy), s_zhi, i)

        def f_zlo(i):
            wait("dve", s_zhi, i)
            free("dve", s_f, i, 3)
            do("dve", lambda e: e.tensor_tensor(zTl[i % 3][:, :, :], z_ps(i), zTh[i % 3][:, :, :], ALU.subtract), s_zlo, i)

        def f_out(i):
            wait("pe", s_zlo, i)
            if i < 2:
                wait("pe", *misc_reader[misc_banks.index(f_bank(i))])
            free("pe", s_out, i, 2)
            for c in range(FC):
                for n, (zz, w) in enumerate(((zTh, T2h), (zTh, T2l), (zTl, T2h))):
                    do("pe", lambda e, c=c, n=n, zz=zz, w=w: e.matmul(
                        f_bank(i)[:, 0:D], zz[i % 3][:, c, :], w[:, c, :], start=(c, n) == (0, 0),
                        stop=(c, n) == (FC - 1, 2)), *((s_f, i) if (c, n) == (FC - 1, 2) else ()))

        def f_sum(i):
            wait("dve", s_f, i)
            wait("dve", s_xb, i)
            do("dve", lambda e: e.scalar_tensor_tensor(X[:, i, :], f_bank(i)[:, 0:D], s_f2[:, :], X[:, i, :],
                                                       ALU.mult, ALU.add), s_out, i)
            if i % STORE == STORE - 1:
                tl = slice(i + 1 - STORE, i + 1)
                wait("sp", s_out, i)
                do("sp", lambda e: e.dma_start(out_tok[:, tl, :], X[:, tl, :]), s_store, i)

        for i in range(2):
            do("dve", lambda e, i=i: e.memset(y[i][:, D - 1:D], 1.0), *((s_dc, "y") if i else ()))
        for eng in ("pe", "pool"):
            wait(eng, s_w, "ffn_weights")
        turns = ((L_NORM, f_norm), (L_HID, f_hidden), (L_ZT, f_zT), (L_OUT, f_out), (L_YT, f_yT),
                 (L_HID, f_gelu), (L_ZT, f_zhi), (L_YT, f_yhi),
                 (L_STAT, f_stats), (L_ZLO, f_zlo), (L_STAT, f_variance), (L_STAT, f_root), (L_STAT, f_negmean),
                 (L_YLO, f_ylo), (0, f_y), (0, f_bias), (L_SUM, f_sum))

        def ffn_turn(t):
            for lag, fn in turns:
                if 0 <= t - lag < NT:
                    fn(t - lag)

        for t in range(NT + L_SUM):
            if t < FFN_LEAD + TAIL:
                attention_step(NH - FFN_LEAD + t)
            ffn_turn(t)
        wait("sp", s_store, NT - 1)

        block = ctx.enter_context(nc.Block())

        @block.sync
        def _(e):
            q.replay("sp", e)

        @block.scalar
        def _(e):
            q.replay("act", e)

        @block.gpsimd
        def _(e):
            q.replay("pool", e)

        @block.vector
        def _(e):
            q.replay("dve", e)

        @block.tensor
        def _(e):
            q.replay("pe", e)


_INS = ["L0_attn_query", "L0_attn_Wq", "L0_attn_Wk", "L0_attn_Wv", "L0_attn_Wp", "L0_attn_bp",
        "L0_ffn_ln1_g", "L0_ffn_ln1_b", "L0_ffn_w1", "L0_ffn_b1", "L0_ffn_ln2_g", "L0_ffn_ln2_b", "L0_ffn_w2", "L0_ffn_b2"]


def kernel(**inputs):
    from concourse import bacc
    from concourse.bass_utils import run_bass_kernel_spmd

    nc = bacc.Bacc("TRN2", target_bir_lowering=False, num_devices=1)
    arrays, args = {}, []
    for name in _INS:
        a = np.ascontiguousarray(inputs[name])
        arrays[f"in_{name}"] = a
        args.append(nc.dram_tensor(f"in_{name}", a.shape, mybir.dt.from_np(a.dtype), kind="ExternalInput").ap())
    result = nc.dram_tensor("result", (B, N, D), F32, kind="ExternalOutput").ap()
    layer(nc, *args, result)
    r = run_bass_kernel_spmd(nc, [arrays], core_ids=[0])
    return r.results[0]["result"]
```
